# Optimizing a Trainium2 kernel written in Bass

```python
import numpy as np
import jax
import jax.numpy as jnp

def _softmax(x, axis=-1):
    return jax.nn.softmax(x, axis=axis)

def _gelu(x):
    return jax.nn.gelu(x, approximate=True)

def _silu(x):
    return jax.nn.silu(x)

def _sigmoid(x):
    return jax.nn.sigmoid(x)

def _layernorm(x, axis=-1, eps=1e-05):
    m = jnp.mean(x, axis=axis, keepdims=True)
    v = jnp.var(x, axis=axis, keepdims=True)
    return (x - m) / jnp.sqrt(v + eps)

def _scatter_add(tgt, idx, src, axis=0):
    return tgt.at[idx].add(src)

def _segment_sum(src, seg, n):
    return jax.ops.segment_sum(src, seg, n)
kernel_name = 'mk_gnn_resnorm_d2_gnn_r32_f206df'

def setup_inputs(seed: int=0):
    np.random.seed(seed)
    _w = jnp.asarray

    def _rec_inputs():
        import jax
        import jax.numpy as jnp
        _gk = jax.random.key(seed)
        x = -0.0004402 + 1 * jax.random.normal(jax.random.fold_in(_gk, 1), (3125, 16), jnp.float32)
        _s = jax.random.randint(jax.random.fold_in(_gk, 2), (50000,), 0, 3125, jnp.int32)
        _d = jax.random.randint(jax.random.fold_in(_gk, 3), (50000,), 0, 3125, jnp.int32)
        _loop = jnp.arange(3125, dtype=jnp.int32)
        src = jnp.concatenate([_s, _d, _loop])
        dst = jnp.concatenate([_d, _s, _loop])
        _o = jnp.argsort(dst, stable=True)
        src = src[_o]
        dst = dst[_o]
        edge_attr_16 = -3.57403e-05 + 0.999761 * jax.random.normal(jax.random.fold_in(_gk, 12), (103125, 16), jnp.float32)
        edge_type_8 = jax.random.randint(jax.random.fold_in(_gk, 14), (103125,), 0, 8, jnp.int32)
        return (x, src, dst, edge_attr_16, edge_type_8)
    x, src, dst, edge_attr_16, edge_type_8 = _rec_inputs()

    def _L0_gnn_setup():
        import jax, jax.numpy as jnp
        import numpy as np
        N_NODES = 30000
        N_EDGES = 9375
        IN_FEATS = 16
        OUT_FEATS = 16
        EDGE_DIM = 16
        key = jax.random.key(seed)
        ks = jax.random.split(key, 8)
        feat = jax.random.normal(ks[0], (N_NODES, IN_FEATS), dtype=jnp.float32)
        efeat = jax.random.normal(ks[1], (N_EDGES, EDGE_DIM), dtype=jnp.float32)
        W_msg = jax.random.normal(ks[2], (EDGE_DIM, IN_FEATS * OUT_FEATS), dtype=jnp.float32) * 0.1
        b_msg = jnp.zeros((IN_FEATS * OUT_FEATS,), dtype=jnp.float32)
        W_attn = jax.random.normal(ks[3], (EDGE_DIM, IN_FEATS * OUT_FEATS), dtype=jnp.float32) * 0.1
        b_attn = jnp.zeros((IN_FEATS * OUT_FEATS,), dtype=jnp.float32)
        src = jax.random.randint(ks[4], (N_EDGES,), 0, N_NODES, dtype=jnp.int32)
        dst = jax.random.randint(ks[5], (N_EDGES,), 0, N_NODES, dtype=jnp.int32)
        return {'feat': feat, 'efeat': efeat, 'W_msg': W_msg, 'b_msg': b_msg, 'W_attn': W_attn, 'b_attn': b_attn, 'src': src, 'dst': dst}
    _L0_gnn_all = _L0_gnn_setup()
    _L0_gnn_in = {k: v for k, v in _L0_gnn_all.items() if k in ('W_msg', 'b_msg', 'W_attn', 'b_attn')}
    del _L0_gnn_all

    def _L1_gnn_setup():
        import jax, jax.numpy as jnp
        import numpy as np
        NUM_ENTITIES = 3125
        NUM_RELATIONS = 8
        NUM_CLASSES = 16
        HIDDEN = 16
        NUM_EDGES = 100000

        def rgcn_conv(x, src, dst, edge_type, W, root, bias):
            num_nodes = x.shape[0]
            x_src = x[src]
            msg = jnp.zeros((src.shape[0], W.shape[2]), x.dtype)
            for r in range(NUM_RELATIONS):
                msg = msg + jnp.where((edge_type == r)[:, None], x_src @ W[r], jnp.zeros((), x.dtype))
            cnt = jnp.zeros((num_nodes, NUM_RELATIONS), x.dtype).at[dst, edge_type].add(1.0)
            norm = 1.0 / jnp.maximum(cnt[dst, edge_type], 1.0)
            agg = jax.ops.segment_sum(msg * norm[:, None], dst, num_segments=num_nodes)
            return agg + x @ root + bias
        key = jax.random.key(seed)
        ks = jax.random.split(key, 9)
        s = 1.0 / np.sqrt(HIDDEN)
        edge_index = jax.random.randint(ks[0], (2, NUM_EDGES), 0, NUM_ENTITIES, dtype=jnp.int32)
        edge_type = jax.random.randint(ks[1], (NUM_EDGES,), 0, NUM_RELATIONS, dtype=jnp.int32)
        return {'embed': jax.random.normal(ks[2], (NUM_ENTITIES, HIDDEN), jnp.float32), 'W1': jax.random.normal(ks[3], (NUM_RELATIONS, HIDDEN, HIDDEN), jnp.float32) * s, 'root1': jax.random.normal(ks[4], (HIDDEN, HIDDEN), jnp.float32) * s, 'b1': jnp.zeros((HIDDEN,), jnp.float32), 'W2': jax.random.normal(ks[5], (NUM_RELATIONS, HIDDEN, NUM_CLASSES), jnp.float32) * s, 'root2': jax.random.normal(ks[6], (HIDDEN, NUM_CLASSES), jnp.float32) * s, 'b2': jnp.zeros((NUM_CLASSES,), jnp.float32), 'edge_index': edge_index, 'edge_type': edge_type}
    _L1_gnn_all = _L1_gnn_setup()
    _L1_gnn_in = {k: v for k, v in _L1_gnn_all.items() if k in ('W1', 'root1', 'b1', 'W2', 'root2', 'b2')}
    del _L1_gnn_all
    return {'x': x, 'src': src, 'dst': dst, 'edge_attr_16': edge_attr_16, 'edge_type_8': edge_type_8, 'L0_gnn_W_msg': _L0_gnn_in['W_msg'], 'L0_gnn_b_msg': _L0_gnn_in['b_msg'], 'L0_gnn_W_attn': _L0_gnn_in['W_attn'], 'L0_gnn_b_attn': _L0_gnn_in['b_attn'], 'L1_gnn_W1': _L1_gnn_in['W1'], 'L1_gnn_root1': _L1_gnn_in['root1'], 'L1_gnn_b1': _L1_gnn_in['b1'], 'L1_gnn_W2': _L1_gnn_in['W2'], 'L1_gnn_root2': _L1_gnn_in['root2'], 'L1_gnn_b2': _L1_gnn_in['b2']}

def reference(x, src, dst, edge_attr_16, edge_type_8, L0_gnn_W_msg, L0_gnn_b_msg, L0_gnn_W_attn, L0_gnn_b_attn, L1_gnn_W1, L1_gnn_root1, L1_gnn_b1, L1_gnn_W2, L1_gnn_root2, L1_gnn_b2):
    import jax
    import jax.numpy as jnp

    def _L0_gnn_ref(feat, efeat, W_msg, b_msg, W_attn, b_attn, src, dst):
        import jax, jax.numpy as jnp
        import numpy as np
        N_NODES = 30000
        N_EDGES = 9375
        IN_FEATS = 16
        OUT_FEATS = 16
        EDGE_DIM = 16
        N, in_f = feat.shape
        E = efeat.shape[0]
        w_m = (efeat @ W_msg + b_msg).reshape(E, in_f, -1)
        w_a = (efeat @ W_attn + b_attn).reshape(E, in_f, -1)
        h_src = feat[src][:, :, None]
        e1 = w_m * h_src
        e2 = w_a * h_src
        seg_max = jax.ops.segment_max(e2, dst, num_segments=N)
        ex = jnp.exp(e2 - seg_max[dst])
        denom = jax.ops.segment_sum(ex, dst, num_segments=N)
        attn = ex / denom[dst]
        ft = jax.ops.segment_sum(e1 * attn, dst, num_segments=N)
        return ft.sum(axis=1)

    def _L1_gnn_ref(embed, W1, root1, b1, W2, root2, b2, edge_index, edge_type):
        import jax, jax.numpy as jnp
        import numpy as np
        NUM_ENTITIES = 3125
        NUM_RELATIONS = 8
        NUM_CLASSES = 16
        HIDDEN = 16
        NUM_EDGES = 100000

        def rgcn_conv(x, src, dst, edge_type, W, root, bias):
            num_nodes = x.shape[0]
            x_src = x[src]
            msg = jnp.zeros((src.shape[0], W.shape[2]), x.dtype)
            for r in range(NUM_RELATIONS):
                msg = msg + jnp.where((edge_type == r)[:, None], x_src @ W[r], jnp.zeros((), x.dtype))
            cnt = jnp.zeros((num_nodes, NUM_RELATIONS), x.dtype).at[dst, edge_type].add(1.0)
            norm = 1.0 / jnp.maximum(cnt[dst, edge_type], 1.0)
            agg = jax.ops.segment_sum(msg * norm[:, None], dst, num_segments=num_nodes)
            return agg + x @ root + bias
        src, dst = (edge_index[0], edge_index[1])
        h = rgcn_conv(embed, src, dst, edge_type, W1, root1, b1)
        h = jax.nn.relu(h)
        h = rgcn_conv(h, src, dst, edge_type, W2, root2, b2)
        return jax.nn.log_softmax(h, axis=1)
    edge_index = jnp.stack([src, dst])
    x = _layernorm(x + _L0_gnn_ref(x, edge_attr_16, L0_gnn_W_msg, L0_gnn_b_msg, L0_gnn_W_attn, L0_gnn_b_attn, src, dst), axis=-1)
    x = _layernorm(x + _L1_gnn_ref(x, L1_gnn_W1, L1_gnn_root1, L1_gnn_b1, L1_gnn_W2, L1_gnn_root2, L1_gnn_b2, edge_index, edge_type_8), axis=-1)
    return x

_drawn_inputs = setup_inputs


def setup_inputs(seed=0):
    import zlib

    import numpy as np

    out = dict(_drawn_inputs(seed))
    spreads = {'L0_gnn_b_msg': (0.0, 0.1),
     'L0_gnn_b_attn': (0.0, 0.1),
     'L1_gnn_b1': (0.0, 0.1),
     'L1_gnn_b2': (0.0, 0.358)}
    factors = {}
    for name, (base, spread) in spreads.items():
        noise = np.random.default_rng([zlib.crc32(name.encode()), seed]).standard_normal(out[name].shape)
        drawn = base * np.exp(spread * noise) if base else spread * noise
        out[name] = jnp.asarray(drawn.astype(out[name].dtype))
    for name, factor in factors.items():
        out[name] = (out[name] * factor).astype(out[name].dtype)
    return out
```

```python
import concourse.bass as bass
from concourse import mybir
from contextlib import ExitStack

F32 = mybir.dt.float32
BF16 = mybir.dt.bfloat16
I32 = mybir.dt.int32
ALU = mybir.AluOpType
ACT = mybir.ActivationFunctionType
X = mybir.AxisListType.X

NODES = 3125
EDGES = 103125
FEATS = 16
RELATIONS = 8
CHANNELS = FEATS * FEATS
EPS = 1e-5

SLOTS = 8
BLOCKS = -(-(NODES + EDGES // SLOTS) // 128)
RING = 3
BLOCKS += -BLOCKS % RING
ROWS = BLOCKS * 128
RUN = SLOTS * FEATS

NP, NB = 125, 25
CUTS, CUT = 275, 375
PIECES = 6
CODED = PIECES * FEATS + 3

LOWEST = -1e37
OFF = -1e30


class Tensors:
    pass


class Chain:

    def __init__(self, eng, sem):
        self.eng, self.sem, self.n = eng, sem, 0

    def __call__(self, instruction):
        instruction.then_inc(self.sem, 1)
        self.n += 1
        self.eng.wait_ge(self.sem, self.n)


def at_least(eng, sem, value):
    if not isinstance(value, int) or value > 0:
        eng.wait_ge(sem, value)




def build(nc, d, out):
    ctx = ExitStack()
    with ctx:
        def sb(name, shape, dt=F32):
            return ctx.enter_context(nc.sbuf_tensor(name, shape, dt))

        def sem(name):
            return ctx.enter_context(nc.semaphore(name))

        def sems(name):
            return [sem(f"{name}{u}") for u in range(RING)]

        m = Tensors()
        m.row_table = nc.dram_tensor("row_table", (ROWS, 4), F32, kind="Internal").ap()
        m.restart_table = nc.dram_tensor("restart_table", (ROWS,), F32, kind="Internal").ap()
        m.row_sums = nc.dram_tensor("row_sums", (ROWS, FEATS), F32, kind="Internal").ap()
        m.projected = [nc.dram_tensor(f"projected{k}", (NODES * RELATIONS, FEATS), F32, kind="Internal").ap() for k in range(2)]
        m.row_aggs = [nc.dram_tensor(f"row_aggs{k}", (ROWS, FEATS), F32, kind="Internal").ap() for k in range(2)]
        m.ident = sb("ident", [128, 128])
        m.ident16 = sb("ident16", [128, 128], BF16)
        m.ones_row = sb("ones_row", [1, 128])
        m.slot_no = sb("slot_no", [128, SLOTS])
        m.out_sel = sb("out_sel", [128, FEATS])
        m.facts = sb("facts", [128, BLOCKS, 1 + SLOTS], I32)
        m.used = sb("used", [128, BLOCKS, SLOTS])
        m.off = sb("off", [128, BLOCKS, SLOTS])
        m.keep = sb("keep", [BLOCKS, 129])
        m.node_last = sb("node_last", [NP, NB], I32)
        m.node_has = sb("node_has", [NP, NB])
        m.edge_ids = sb("edge_ids", [128, BLOCKS, SLOTS, 2], I32)
        m.coded_w = sb("coded_w", [CODED, 2 * CHANNELS], BF16)
        m.node_x = sb("node_x", [NP, NB, FEATS])
        m.norm = sb("norm", [128, BLOCKS, SLOTS])
        m.message_at = sb("message_at", [128, BLOCKS, SLOTS], I32)
        m.messages = sb("messages", [128, FEATS, BLOCKS])
        m.hidden = sb("hidden", [NP, NB, FEATS])
        m.rooted = sb("rooted", [NP, NB, FEATS])
        m.psum = [ctx.enter_context(nc.psum_tensor(f"bank{i}", [128, 512], F32)) for i in range(8)]
        m.coded = [sb(f"coded{u}", [128, SLOTS, CODED], BF16) for u in range(RING)]
        m.peak = [sb(f"run_peak{u}", [128, 2, 129]) for u in range(RING)]
        m.carried = [sb(f"carried{u}", [128, 4, 128]) for u in range(RING)]

        make_rows(nc, d, m, sem)
        attention(nc, d, m, sem, sems)
        finish_attention(nc, d, m, sem)
        relation_norms(nc, d, m, sem)
        for k in range(2):
            project(nc, d, m, sem, k)
            gather_messages(nc, m, sem, sems, k)
            segment_sums(nc, m, sem, m.messages, FEATS, m.row_aggs[k], f"agg{k}")
            finish_layer(nc, d, m, sem, k, out)


def make_rows(nc, d, m, sem):
    ctx = ExitStack()
    with ctx:
        def sb(name, shape, dt=F32):
            return ctx.enter_context(nc.sbuf_tensor(name, shape, dt))

        heads_i = sb("heads_i", [1, CUTS], I32)
        heads = sb("heads", [1, CUTS])
        node_i = sb("node_i", [NP, NB + 1], I32)
        node_no = sb("node_no", [NP, NB + 1])
        before = sb("before", [NP, NB + 1, CUT])
        piece = sb("piece", [NP, NB + 1, CUT], I32)
        cut_no = sb("cut_no", [NP, NB + 1])
        cut_i = sb("cut_i", [NP, NB + 1], I32)
        inside = sb("inside", [NP, NB + 1])
        start = sb("start", [NP, NB + 1])
        upto_i = sb("upto_i", [NP, NB], I32)
        count = sb("count", [NP, NB])
        last = sb("last", [NP, NB])
        base = sb("base", [NP, 1])
        ones = sb("ones", [NP, NB])
        earlier = sb("earlier", [NP, NP])
        to_row = sb("to_row", [NP, NB])
        to_row_i = sb("to_row_i", [NP, NB], I32)
        entry = sb("entry", [NP, NB, 4])
        zeros = sb("zeros", [BLOCKS, 512])
        table = sb("table", [BLOCKS, 128, 4])
        filled = sb("filled", [BLOCKS, 4, 128])
        ends = sb("ends", [BLOCKS, 4])
        carry_t = sb("carry_t", [4, BLOCKS + 1])
        carry = sb("carry", [BLOCKS, 4])
        row_i = sb("row_i", [BLOCKS, 128], I32)
        row_no = sb("row_no", [BLOCKS, 128])
        first = sb("first", [BLOCKS, 128])
        begin = sb("begin", [BLOCKS, 128])
        length = sb("length", [BLOCKS, 128])
        restart = sb("restart", [BLOCKS, 128])
        length_t = sb("length_t", [128, BLOCKS])
        slot_i = sb("slot_i", [128, SLOTS], I32)
        picks = sb("picks", [128, FEATS, FEATS])
        w_in = sb("w_in", [FEATS, 2 * CHANNELS])
        b_in = sb("b_in", [1, 2 * CHANNELS])
        w_rest = sb("w_rest", [FEATS, 2 * CHANNELS])
        b_rest = sb("b_rest", [1, 2 * CHANNELS])
        w_parts = sb("w_parts", [FEATS, 3, 2 * CHANNELS], BF16)
        b_parts = sb("b_parts", [1, 3, 2 * CHANNELS], BF16)

        heads_in, weights_in, table_clear, x_in = sem("heads_in"), sem("weights_in"), sem("table_clear"), sem("x_in")
        table_in, restart_out, coded_w_in = sem("table_in"), sem("restart_out"), sem("coded_w_in")
        pool_chain, vec_chain = sem("rows_pool_chain"), sem("rows_vec_chain")
        constants, heads_ready, heads_spread = sem("constants"), sem("heads_ready"), sem("heads_spread")
        cuts_ready, pieces_in, totals_ready, bases_ready = sem("cuts_ready"), sem("pieces_in"), sem("totals_ready"), sem("bases_ready")
        entries_ready, entries_out, zeros_ready = sem("entries_ready"), sem("entries_out"), sem("zeros_ready")
        ends_ready, ends_turned, carry_ready, carry_turned = sem("ends_ready"), sem("ends_turned"), sem("carry_ready"), sem("carry_turned")
        rows_ready, rows_turned, parts_ready = sem("rows_ready"), sem("rows_turned"), sem("parts_ready")

        heads_ps, base_ps = m.psum[0][0:NP, 0:CUTS], m.psum[1][0:NP, 0:1]
        ends_ps, carry_ps = m.psum[2][0:4, 0:BLOCKS], m.psum[3][0:BLOCKS, 0:4]
        begin_ps, length_ps = m.psum[4][:, 0:BLOCKS], m.psum[5][:, 0:BLOCKS]

        with nc.Block() as block:
            @block.sync
            def _(sp):
                with nc.allow_non_contiguous_dma(reason="one destination in each piece"):
                    sp.dma_start(heads_i[:, :], d.dst.rearrange("(a c) -> a c", c=CUT)[:, 0:1].rearrange("a c -> c a")).then_inc(heads_in, 16)
                sp.dma_start(w_in[:, 0:CHANNELS], d.w_attn).then_inc(weights_in, 16)
                sp.dma_start(w_in[:, CHANNELS:], d.w_msg).then_inc(weights_in, 16)
                sp.dma_start(b_in[:, 0:CHANNELS], d.b_attn.rearrange("(a n) -> a n", a=1)).then_inc(weights_in, 16)
                sp.dma_start(b_in[:, CHANNELS:], d.b_msg.rearrange("(a n) -> a n", a=1)).then_inc(weights_in, 16)
                sp.dma_start(m.node_x[:, :, :], d.x.rearrange("(p b) f -> p b f", b=NB)).then_inc(x_in, 16)
                sp.wait_ge(zeros_ready, 1)
                sp.dma_start(m.row_table.rearrange("(p r) c -> p (r c)", r=128), zeros[:, :]).then_inc(table_clear, 16)
                sp.wait_ge(parts_ready, 1)
                for row, part in enumerate((0, 1, 2, 0, 1, 0)):
                    sp.dma_start(m.coded_w[row * FEATS:(row + 1) * FEATS, :], w_parts[:, part, :]).then_inc(coded_w_in, 16)
                for part in range(3):
                    sp.dma_start(m.coded_w[PIECES * FEATS + part:PIECES * FEATS + part + 1, :], b_parts[:, part, :]).then_inc(coded_w_in, 16)
                sp.wait_ge(entries_out, 16 * NB)
                sp.dma_start(table[:, :, :], m.row_table.rearrange("(p r) c -> p r c", r=128)).then_inc(table_in, 16)
                sp.wait_ge(rows_ready, 1)
                sp.dma_start(m.restart_table.rearrange("(p r) -> p r", r=128), restart[:, :]).then_inc(restart_out, 16)
                sp.wait_ge(restart_out, 16)
                sp.wait_ge(coded_w_in, 16 * (PIECES + 3))
                sp.wait_ge(x_in, 16)

            @block.gpsimd
            def _(pool):
                chain = Chain(pool, pool_chain)
                nc.gpsimd.memset(zeros[:, :], 0.0).then_inc(zeros_ready, 1)
                chain(nc.gpsimd.iota(node_i[:, :], pattern=[[1, NB + 1]], base=0, channel_multiplier=NB))
                chain(nc.gpsimd.iota(row_i[:, :], pattern=[[1, 128]], base=0, channel_multiplier=128))
                chain(nc.gpsimd.iota(slot_i[:, :], pattern=[[1, SLOTS]], base=0, channel_multiplier=0))
                chain(nc.gpsimd.memset(m.ident[:, :], 0.0))
                chain(nc.gpsimd.memset(m.ones_row[:, :], 1.0))
                chain(nc.gpsimd.memset(ones[:, :], 1.0))
                chain(nc.gpsimd.memset(earlier[:, :], 1.0))
                chain(nc.gpsimd.memset(picks[:, :, :], 0.0))
                chain(nc.gpsimd.affine_select(out=m.ident[:, :], in_=m.ident[:, :], compare_op=ALU.not_equal, fill=1.0,
                                              base=0, pattern=[[-1, 128]], channel_multiplier=1))
                chain(nc.gpsimd.affine_select(out=earlier[:, :], in_=earlier[:, :], compare_op=ALU.is_gt, fill=0.0,
                                              base=0, pattern=[[1, NP]], channel_multiplier=-1))
                chain(nc.gpsimd.affine_select(out=picks[:, :, :], in_=picks[:, :, :], compare_op=ALU.not_equal, fill=1.0,
                                              base=0, pattern=[[-FEATS, FEATS], [-1, FEATS]], channel_multiplier=1))
                for u in range(RING):
                    chain(nc.gpsimd.memset(m.coded[u][:, :, PIECES * FEATS:CODED], 1.0))
                chain(nc.gpsimd.memset(m.peak[RING - 1][:, :, 128:129], LOWEST))
                chain(nc.gpsimd.memset(m.carried[RING - 1][:, :, :], 0.0))
                nc.gpsimd.memset(m.keep[:, 128:129], 1.0).then_inc(constants, 1)
                pool.wait_ge(cuts_ready, 1)
                for b in range(NB + 1):
                    pool.indirect_dma_start(piece[:, b, :], None, d.dst.rearrange("(a c) -> a c", c=CUT),
                                            bass.IndirectOffsetOnAxis(cut_i[:, b:b + 1], 0)).then_inc(pieces_in, 16)
                pool.wait_ge(entries_ready, 1)
                pool.wait_ge(table_clear, 16)
                for b in range(NB):
                    pool.indirect_dma_start(m.row_table, bass.IndirectOffsetOnAxis(to_row_i[:, b:b + 1], 0), entry[:, b, :], None,
                                            bounds_check=ROWS - 1, oob_is_err=False).then_inc(entries_out, 16)
                pool.wait_ge(entries_out, 16 * NB)

            @block.tensor
            def _(pe):
                pe.wait_ge(constants, 1)
                pe.wait_ge(heads_ready, 1)
                nc.tensor.matmul(heads_ps, m.ones_row[:, 0:NP], heads[:, :], start=True, stop=True).then_inc(heads_spread, 1)
                pe.wait_ge(totals_ready, 1)
                nc.tensor.matmul(base_ps, earlier[:, :], last[:, NB - 1:NB], start=True, stop=True).then_inc(bases_ready, 1)
                pe.wait_ge(ends_ready, 1)
                nc.tensor.transpose(ends_ps, ends[:, :], m.ident[0:BLOCKS, 0:BLOCKS]).then_inc(ends_turned, 1)
                pe.wait_ge(carry_ready, 1)
                nc.tensor.transpose(carry_ps, carry_t[:, 0:BLOCKS], m.ident[0:4, 0:4]).then_inc(carry_turned, 1)
                pe.wait_ge(rows_ready, 1)
                nc.tensor.transpose(begin_ps, begin[:, :], m.ident[0:BLOCKS, 0:BLOCKS]).then_inc(rows_turned, 1)
                nc.tensor.transpose(length_ps, length[:, :], m.ident[0:BLOCKS, 0:BLOCKS]).then_inc(rows_turned, 1)

            @block.vector
            def _(dve):
                chain = Chain(dve, vec_chain)
                v = nc.vector
                dve.wait_ge(heads_in, 16)
                v.tensor_copy(heads[:, :], heads_i[:, :]).then_inc(heads_ready, 1)
                dve.wait_ge(constants, 1)
                chain(v.tensor_copy(node_no[:, :], node_i[:, :]))
                chain(v.tensor_copy(row_no[:, :], row_i[:, :]))
                chain(v.tensor_copy(m.slot_no[:, :], slot_i[:, :]))
                chain(v.tensor_copy(m.ident16[:, :], m.ident[:, :]))
                chain(v.tensor_reduce(m.out_sel[:, :], picks[:, :, :].rearrange("c i o -> c o i"), X, ALU.add))
                dve.wait_ge(heads_spread, 1)
                chain(v.tensor_tensor(before[:, :, 0:CUTS], heads_ps.unsqueeze(1).broadcast_to([NP, NB + 1, CUTS]),
                                      node_no[:, :].unsqueeze(2).broadcast_to([NP, NB + 1, CUTS]), ALU.is_lt))
                chain(v.tensor_reduce(cut_no[:, :], before[:, :, 0:CUTS], X, ALU.add))
                chain(v.tensor_scalar(cut_no[:, :], cut_no[:, :], -1.0, 0.0, ALU.add, ALU.max))
                v.tensor_copy(cut_i[:, :], cut_no[:, :]).then_inc(cuts_ready, 1)
                dve.wait_ge(weights_in, 64)
                for whole, rest, parts in ((w_in, w_rest, w_parts), (b_in, b_rest, b_parts)):
                    chain(v.tensor_copy(parts[:, 0, :], whole[:, :]))
                    chain(v.tensor_tensor(rest[:, :], whole[:, :], parts[:, 0, :], ALU.subtract))
                    chain(v.tensor_copy(parts[:, 1, :], rest[:, :]))
                    chain(v.tensor_tensor(rest[:, :], rest[:, :], parts[:, 1, :], ALU.subtract))
                    if parts is w_parts:
                        chain(v.tensor_copy(parts[:, 2, :], rest[:, :]))
                v.tensor_copy(b_parts[:, 2, :], b_rest[:, :]).then_inc(parts_ready, 1)
                dve.wait_ge(pieces_in, 16 * (NB + 1))
                chain(v.tensor_tensor(before[:, :, :], piece[:, :, :], node_no[:, :].unsqueeze(2).broadcast_to([NP, NB + 1, CUT]), ALU.is_lt))
                chain(v.tensor_reduce(inside[:, :], before[:, :, :], X, ALU.add))
                chain(v.scalar_tensor_tensor(start[:, :], cut_no[:, :], float(CUT), inside[:, :], ALU.mult, ALU.add))
                chain(v.tensor_tensor(count[:, :], start[:, 1:NB + 1], start[:, 0:NB], ALU.subtract))
                chain(v.tensor_scalar(upto_i[:, :], count[:, :], float(SLOTS - 1), None, ALU.add))
                chain(v.tensor_scalar(upto_i[:, :], upto_i[:, :], SLOTS.bit_length() - 1, None, ALU.arith_shift_right))
                chain(v.tensor_copy(count[:, :], upto_i[:, :]))
                v.tensor_tensor_scan(last[:, :], ones[:, :], count[:, :], 0.0, ALU.mult, ALU.add).then_inc(totals_ready, 1)
                dve.wait_ge(bases_ready, 1)
                chain(v.tensor_copy(base[:, :], base_ps))
                chain(v.tensor_scalar(last[:, :], last[:, :], base[:, :], None, ALU.add))
                chain(v.tensor_scalar(m.node_has[:, :], count[:, :], 0.0, None, ALU.is_gt))
                chain(v.tensor_copy(entry[:, :, 0], start[:, 0:NB]))
                chain(v.tensor_copy(entry[:, :, 1], start[:, 1:NB + 1]))
                chain(v.tensor_tensor(entry[:, :, 2], last[:, :], count[:, :], ALU.subtract))
                chain(v.tensor_scalar(entry[:, :, 3], node_no[:, 0:NB], 1.0, None, ALU.add))
                chain(v.tensor_scalar(to_row[:, :], m.node_has[:, :], -2.0 * ROWS, 2.0 * ROWS, ALU.mult, ALU.add))
                chain(v.tensor_tensor(to_row[:, :], to_row[:, :], entry[:, :, 2], ALU.add))
                chain(v.tensor_copy(to_row_i[:, :], to_row[:, :]))
                chain(v.tensor_scalar(last[:, :], last[:, :], -1.0, 0.0, ALU.add, ALU.max))
                v.tensor_copy(m.node_last[:, :], last[:, :]).then_inc(entries_ready, 1)
                dve.wait_ge(table_in, 16)
                for c in range(4):
                    chain(v.tensor_tensor_scan(filled[:, c, :], table[:, :, c], table[:, :, c], 0.0, ALU.max, ALU.max))
                chain(v.memset(carry_t[:, 0:1], 0.0))
                v.tensor_copy(ends[:, :], filled[:, :, 127]).then_inc(ends_ready, 1)
                dve.wait_ge(ends_turned, 1)
                chain(v.tensor_copy(carry_t[:, 1:BLOCKS + 1], ends_ps))
                v.tensor_tensor_scan(carry_t[:, 1:BLOCKS + 1], carry_t[:, 1:BLOCKS + 1], carry_t[:, 1:BLOCKS + 1], 0.0,
                                     ALU.max, ALU.max).then_inc(carry_ready, 1)
                dve.wait_ge(carry_turned, 1)
                chain(v.tensor_copy(carry[:, :], carry_ps))
                for c in range(3):
                    chain(v.tensor_scalar(filled[:, c, :], filled[:, c, :], carry[:, c:c + 1], None, ALU.max))
                chain(v.tensor_tensor(row_no[:, :], row_no[:, :], filled[:, 2, :], ALU.subtract))
                chain(v.scalar_tensor_tensor(begin[:, :], row_no[:, :], float(SLOTS), filled[:, 0, :], ALU.mult, ALU.add))
                chain(v.tensor_scalar(begin[:, :], begin[:, :], float(EDGES), None, ALU.min))
                chain(v.tensor_tensor(length[:, :], filled[:, 1, :], begin[:, :], ALU.subtract))
                chain(v.tensor_scalar(first[:, :], table[:, :, 3], 0.0, None, ALU.is_gt))
                chain(v.tensor_scalar(m.keep[:, 0:128], first[:, :], -1.0, 1.0, ALU.mult, ALU.add))
                v.tensor_scalar(restart[:, :], first[:, :], LOWEST, None, ALU.mult).then_inc(rows_ready, 1)
                dve.wait_ge(rows_turned, 2)
                chain(v.tensor_copy(m.facts[:, :, 0], begin_ps))
                chain(v.tensor_copy(length_t[:, :], length_ps))
                chain(v.tensor_tensor(m.used[:, :, :], m.slot_no[:, :].unsqueeze(1).broadcast_to([128, BLOCKS, SLOTS]),
                                      length_t[:, :].unsqueeze(2).broadcast_to([128, BLOCKS, SLOTS]), ALU.is_lt))
                chain(v.tensor_scalar(m.facts[:, :, 1:1 + SLOTS], m.used[:, :, :], -1.0, 1.0, ALU.mult, ALU.add))
                chain(v.tensor_scalar(m.off[:, :, :], m.used[:, :, :], -OFF, OFF, ALU.mult, ALU.add))


def attention(nc, d, m, sem, sems):
    ctx = ExitStack()
    with ctx:
        def ring(name, shape, dt=F32):
            return [ctx.enter_context(nc.sbuf_tensor(f"{name}{u}", shape, dt)) for u in range(RING)]

        facts = ring("facts_at", [128, 1 + SLOTS], I32)
        ids = ring("ids", [128, SLOTS, 2], I32)
        feats = ring("feats", [128, SLOTS, FEATS])
        rest = ring("rest", [128, SLOTS, FEATS])
        sources = ring("sources", [128, SLOTS, FEATS])
        turned = ring("turned_feats", [CODED, SLOTS, 128], BF16)
        pair = ring("pair", [128, SLOTS, 2, CHANNELS])
        row_peak = ring("row_peak", [128, CHANNELS])
        sums = ring("sums", [128, 2 * CHANNELS])
        restart = ring("restart_at", [128, 128])
        below = ring("below", [128, 2, 128])
        drop = ring("drop", [128, 2, 128])
        scaled = ring("scaled", [128, 4, 128])
        ratio = ring("ratio", [128, 2, 128])
        part = ring("row_out", [128, FEATS])

        pair_ps = m.psum[0:4]
        turn_ps = m.psum[4][0:CODED, :].bitcast(BF16).rearrange("p (s r) -> p s r", s=SLOTS)
        sums_ps = m.psum[5]
        sums_t_ps = m.psum[6][:, :].rearrange("p (k r) -> p k r", k=4)
        peak_t_ps = m.psum[7][:, 0:256].rearrange("p (k r) -> p k r", k=2)
        out_ps = m.psum[7][:, 256:256 + FEATS]

        facts_ready, runs_in, picked, kept = sem("facts_ready"), sems("runs_in"), sem("picked"), sem("kept")
        sources_in, high_ready, high_off = sems("sources_in"), sem("high_ready"), sem("high_off")
        mid_ready, mid_off, low_ready = sem("mid_ready"), sem("mid_off"), sem("low_ready")
        feats_turned, feats_ready, weights_made = sem("feats_turned"), sem("feats_ready"), sem("weights_made")
        pair_made, row_peaked, shifted, raised = sem("pair_made"), sem("row_peaked"), sem("shifted"), sem("raised")
        weighed, summed, sums_ready, sums_turned = sem("weighed"), sem("summed"), sem("sums_ready"), sem("sums_turned")
        restart_in, peak_run, below_ready, restarted = sems("restart_in"), sem("peak_run"), sem("below_ready"), sem("restarted")
        drop_ready, below_raised, drop_raised = sem("drop_ready"), sem("below_raised"), sem("drop_raised")
        sums_scaled, joined, inverted, ratio_ready = sem("sums_scaled"), sem("joined"), sem("inverted"), sem("ratio_ready")
        pool_passed, dve_passed = sem("pool_passed"), sem("dve_passed")
        folded, out_ready, out_stored = sem("folded"), sem("out_ready"), sems("out_stored")

        def shifted_by(q, u, by):
            w = u + by
            q, u = q + w // RING, w % RING
            return q, u, q * RING + u

        def is_block(n):
            return not isinstance(n, int) or 0 <= n < BLOCKS

        LOOP = (2, (BLOCKS - 3) // RING)

        def steps(eng, step):
            for n in range(-RING, RING * LOOP[0]):
                step(n // RING, n % RING)
            with eng.Fori(*LOOP) as q:
                for u in range(RING):
                    step(q, u)
            for n in range(RING * LOOP[1], BLOCKS + 4):
                step(n // RING, n % RING)

        with nc.Block() as block:
            @block.sync
            def _(sp):
                def step(q, u):
                    q3, u3, n3 = shifted_by(q, u, -2)
                    if is_block(n3):
                        at_least(sp, drop_ready, n3 - 2)
                        sp.dma_start(restart[u3][:, :], m.restart_table[bass.ds(n3 * 128, 128)].partition_broadcast(128)).then_inc(restart_in[u3], 16)
                    q4, u4, n4 = shifted_by(q, u, -4)
                    if is_block(n4):
                        sp.wait_ge(out_ready, n4 + 1)
                        sp.dma_start(m.row_sums[bass.ds(n4 * 128, 128), :], part[u4][:, :]).then_inc(out_stored[u4], 16)
                steps(sp, step)
                for u in range(RING):
                    sp.wait_ge(out_stored[u], 16 * (BLOCKS // RING))

            @block.gpsimd
            def _(pool):
                g = nc.gpsimd

                def step(q, u):
                    q1, u1, n1 = shifted_by(q, u, 1)
                    q3, u3, n3 = shifted_by(q, u, -3)
                    qa, ua, na = shifted_by(q, u, 3)

                    def gather(slots):
                        for s in slots:
                            pool.indirect_dma_start(sources[u1][:, s, :], None, d.x, bass.IndirectOffsetOnAxis(ids[u1][:, s, 0:1], 0)).then_inc(sources_in[u1], 16)

                    if is_block(n1):
                        pool.wait_ge(picked, 2 * n1 + 2)
                        at_least(pool, pair_made, SLOTS * (n1 - 2))
                        pool.sem_inc(pool_passed, 1)
                        gather(range(0, SLOTS // 2))
                    if is_block(n3):
                        pool.wait_ge(peak_run, 3 * n3 + 3)
                        pool.wait_ge(restart_in[u3], 16 * q3 + 16)
                        at_least(pool, joined, n3 - 2)
                        g.tensor_tensor(drop[u3][:, :, :], m.peak[u3][:, :, 0:128],
                                        restart[u3][:, :].unsqueeze(1).broadcast_to([128, 2, 128]), ALU.add).then_inc(restarted, 1)
                        pool.wait_ge(restarted, n3 + 1)
                        g.tensor_tensor(drop[u3][:, :, :], drop[u3][:, :, :], m.peak[u3][:, :, 1:129], ALU.subtract).then_inc(drop_ready, 1)
                    if is_block(n1):
                        pool.wait_ge(high_ready, n1 + 1)
                        at_least(pool, low_ready, n1 - 2)
                        g.tensor_tensor(rest[u1][:, :, :], feats[u1][:, :, :], m.coded[u1][:, :, 0:FEATS], ALU.subtract).then_inc(high_off, 1)
                        gather(range(SLOTS // 2, SLOTS))
                        pool.wait_ge(mid_ready, n1 + 1)
                        g.tensor_tensor(rest[u1][:, :, :], rest[u1][:, :, :], m.coded[u1][:, :, 3 * FEATS:4 * FEATS], ALU.subtract).then_inc(mid_off, 1)
                    if is_block(na):
                        at_least(pool, runs_in[ua], 32 * qa)
                        at_least(pool, picked, 2 * (na - 2))
                        g.tensor_copy(facts[ua][:, :], m.facts[:, bass.ds(na, 1), :].rearrange("p a c -> p (a c)")).then_inc(facts_ready, 1)
                        pool.wait_ge(facts_ready, na + 1)
                        at_least(pool, sources_in[ua], SLOTS * 16 * qa)
                        at_least(pool, kept, na - 2)
                        at_least(pool, high_ready, na - 2)
                        at_least(pool, high_off, na - 2)
                        pool.sem_inc(pool_passed, 1)
                        pool.indirect_dma_start(ids[ua][:, :, :].rearrange("p s c -> p (s c)"), None, d.ids,
                                                bass.IndirectOffsetOnAxis(facts[ua][:, 0:1], 0)).then_inc(runs_in[ua], 16)
                        pool.indirect_dma_start(feats[ua][:, :, :].rearrange("p s f -> p (s f)"), None, d.efeat,
                                                bass.IndirectOffsetOnAxis(facts[ua][:, 0:1], 0)).then_inc(runs_in[ua], 16)
                steps(pool, step)

            @block.scalar
            def _(act):
                a = nc.scalar

                def step(q, u):
                    q1, u1, n1 = shifted_by(q, u, 1)
                    q3, u3, n3 = shifted_by(q, u, -3)
                    q4, u4, n4 = shifted_by(q, u, -4)
                    n = q * RING + u
                    if is_block(n3):
                        act.wait_ge(summed, n3 + 1)
                        at_least(act, sums_turned, n3 - 2)
                        a.activation(sums[u3][:, :], sums_ps[:, :], ACT.Copy).then_inc(sums_ready, 1)
                    if is_block(n1):
                        act.wait_ge(picked, 2 * n1 + 2)
                        at_least(act, feats_turned, n1 - 2)
                        a.activation(m.coded[u1][:, :, 0:3 * FEATS].rearrange("p s (c f) -> p s c f", f=FEATS),
                                     feats[u1][:, :, :].unsqueeze(2).broadcast_to([128, SLOTS, 3, FEATS]), ACT.Copy).then_inc(high_ready, 1)
                        act.wait_ge(high_off, n1 + 1)
                        a.activation(m.coded[u1][:, :, 3 * FEATS:5 * FEATS].rearrange("p s (c f) -> p s c f", f=FEATS),
                                     rest[u1][:, :, :].unsqueeze(2).broadcast_to([128, SLOTS, 2, FEATS]), ACT.Copy).then_inc(mid_ready, 1)
                        act.wait_ge(mid_off, n1 + 1)
                        a.activation(m.coded[u1][:, :, 5 * FEATS:6 * FEATS], rest[u1][:, :, :], ACT.Copy).then_inc(low_ready, 1)
                        act.wait_ge(feats_turned, n1 + 1)
                        at_least(act, weights_made, SLOTS * (n1 - 2))
                        a.activation(turned[u1][:, :, :], turn_ps, ACT.Copy).then_inc(feats_ready, 1)
                    if is_block(n3):
                        act.wait_ge(below_ready, n3 + 1)
                        a.activation(below[u3][:, :, :], below[u3][:, :, :], ACT.Exp).then_inc(below_raised, 1)
                        act.wait_ge(drop_ready, n3 + 1)
                        a.activation(drop[u3][:, :, :], drop[u3][:, :, :], ACT.Exp).then_inc(drop_raised, 1)
                    if is_block(n):
                        act.wait_ge(shifted, n + 1)
                        for s in range(SLOTS):
                            ex = pair[u][:, s, 0, :]
                            off = m.off[:, bass.ds(n, 1), s]
                            a.activation(ex, ex, ACT.Exp, bias=off).then_inc(raised, 1)
                    if is_block(n4):
                        act.wait_ge(folded, n4 + 1)
                        at_least(act, out_stored[u4], 16 * q4)
                        a.activation(part[u4][:, :], out_ps, ACT.Copy).then_inc(out_ready, 1)
                steps(act, step)

            @block.tensor
            def _(pe):
                t = nc.tensor

                def step(q, u):
                    q1, u1, n1 = shifted_by(q, u, 1)
                    q2, u2, n2 = shifted_by(q, u, -2)
                    q3, u3, n3 = shifted_by(q, u, -3)
                    q4, u4, n4 = shifted_by(q, u, -4)
                    n = q * RING + u
                    if is_block(n):
                        pe.wait_ge(feats_ready, n + 1)
                        for s in range(SLOTS):
                            at_least(pe, pair_made, n * SLOTS + s - 3)
                            t.matmul(pair_ps[s % 4][:, :], turned[u][:, s, :], m.coded_w[:, :], start=True, stop=True).then_inc(weights_made, 1)
                    if is_block(n3):
                        at_least(pe, below_ready, n3)
                        at_least(pe, out_ready, n3 - 1)
                        for h in range(2):
                            t.transpose(peak_t_ps[:, h, :], row_peak[u3][:, h * 128:(h + 1) * 128], m.ident[:, :])
                        pe.wait_ge(sums_ready, n3 + 1)
                        at_least(pe, sums_scaled, n3)
                        for k in range(4):
                            last = t.transpose(sums_t_ps[:, k, :], sums[u3][:, k * 128:(k + 1) * 128], m.ident[:, :])
                        last.then_inc(sums_turned, 1)
                    if is_block(n1):
                        pe.wait_ge(low_ready, n1 + 1)
                        at_least(pe, feats_ready, n1)
                        for s in range(SLOTS):
                            last = t.transpose(turn_ps[:, s, :], m.coded[u1][:, s, :], m.ident16[:, :])
                        last.then_inc(feats_turned, 1)
                    if is_block(n2):
                        pe.wait_ge(weighed, n2 + 1)
                        at_least(pe, sums_ready, n2)
                        for s in range(SLOTS):
                            last = t.matmul(sums_ps[:, :], m.ident[:, :], pair[u2][:, s, :, :].rearrange("p c n -> p (c n)"),
                                            start=(s == 0), stop=(s == SLOTS - 1))
                        last.then_inc(summed, 1)
                    if is_block(n4):
                        pe.wait_ge(ratio_ready, n4 + 1)
                        at_least(pe, out_ready, n4)
                        at_least(pe, below_ready, n3 + 1 if is_block(n3) else n4 + 1)
                        for h in range(2):
                            last = t.matmul(out_ps, ratio[u4][:, h, :], m.out_sel[:, :], start=(h == 0), stop=(h == 1))
                        last.then_inc(folded, 1)
                steps(pe, step)

            @block.vector
            def _(dve):
                v = nc.vector

                def step(q, u):
                    q2, u2, n2 = shifted_by(q, u, 2)
                    q1, u1, n1 = shifted_by(q, u, -1)
                    q3, u3, n3 = shifted_by(q, u, -3)
                    n = q * RING + u
                    if is_block(n2):
                        dve.wait_ge(runs_in[u2], 32 * q2 + 32)
                        dve.wait_ge(facts_ready, n2 + 1)
                        dve.sem_inc(dve_passed, 1)
                        free = facts[u2][:, 2:1 + SLOTS].unsqueeze(2)
                        v.copy_predicated(ids[u2][:, 1:SLOTS, :], free.broadcast_to([128, SLOTS - 1, 2]),
                                          ids[u2][:, 0:1, :].broadcast_to([128, SLOTS - 1, 2])).then_inc(picked, 1)
                        v.copy_predicated(feats[u2][:, 1:SLOTS, :], free.broadcast_to([128, SLOTS - 1, FEATS]),
                                          feats[u2][:, 0:1, :].broadcast_to([128, SLOTS - 1, FEATS])).then_inc(picked, 1)
                        dve.wait_ge(picked, 2 * n2 + 1)
                        v.tensor_copy(m.edge_ids[:, bass.ds(n2, 1), :, :].rearrange("p a s c -> p (a s c)"),
                                      ids[u2][:, :, :].rearrange("p s c -> p (s c)")).then_inc(kept, 1)
                    if is_block(n):
                        dve.wait_ge(sources_in[u], SLOTS * 16 * q + SLOTS * 16)
                        at_least(dve, summed, n - 2)
                        for s in range(SLOTS):
                            dve.wait_ge(weights_made, SLOTS * n + s + 1)
                            v.tensor_tensor(pair[u][:, s, :, :].rearrange("p c (i o) -> p c i o", o=FEATS),
                                            pair_ps[s % 4][:, :].rearrange("p (c i o) -> p c i o", c=2, o=FEATS),
                                            sources[u][:, s, :].unsqueeze(1).unsqueeze(3).broadcast_to([128, 2, FEATS, FEATS]),
                                            ALU.mult).then_inc(pair_made, 1)
                    if is_block(n3):
                        dve.wait_ge(sums_turned, n3 + 1)
                        dve.wait_ge(restart_in[u3], 16 * q3 + 16)
                        at_least(dve, drop_ready, n3 - 2)
                        before = m.peak[(u3 - 1) % RING]
                        at_least(dve, peak_run, 3 * n3)
                        at_least(dve, below_ready, n3 - 2)
                        v.tensor_copy(m.peak[u3][:, :, 0:1], before[:, :, 128:129]).then_inc(peak_run, 1)
                        for h in range(2):
                            v.tensor_tensor_scan(m.peak[u3][:, h, 1:129], restart[u3][:, :], peak_t_ps[:, h, :],
                                                 before[:, h, 128:129], ALU.add, ALU.max).then_inc(peak_run, 1)
                        at_least(dve, sums_scaled, n3 - 2)
                    if is_block(n):
                        dve.wait_ge(pair_made, SLOTS * n + SLOTS)
                        at_least(dve, sums_turned, n - 2)
                        v.tensor_reduce(row_peak[u][:, :], pair[u][:, :, 0, :].rearrange("p s c -> p c s"), X, ALU.max).then_inc(row_peaked, 1)
                    if is_block(n3):
                        dve.wait_ge(peak_run, 3 * n3 + 3)
                        v.tensor_tensor(below[u3][:, :, :], peak_t_ps, m.peak[u3][:, :, 1:129], ALU.subtract).then_inc(below_ready, 1)
                    if is_block(n):
                        dve.wait_ge(row_peaked, n + 1)
                        v.tensor_tensor(pair[u][:, :, 0, :], pair[u][:, :, 0, :],
                                        row_peak[u][:, :].unsqueeze(1).broadcast_to([128, SLOTS, CHANNELS]), ALU.subtract).then_inc(shifted, 1)
                    if is_block(n1):
                        dve.wait_ge(raised, SLOTS * n1 + SLOTS)
                        v.tensor_tensor(pair[u1][:, :, 1, :], pair[u1][:, :, 1, :], pair[u1][:, :, 0, :], ALU.mult).then_inc(weighed, 1)
                    if is_block(n3):
                        dve.wait_ge(below_raised, n3 + 1)
                        v.tensor_tensor(scaled[u3][:, :, :].rearrange("p (c h) r -> p c h r", h=2),
                                        sums_t_ps.rearrange("p (c h) r -> p c h r", h=2),
                                        below[u3][:, :, :].unsqueeze(1).broadcast_to([128, 2, 2, 128]), ALU.mult).then_inc(sums_scaled, 1)
                        dve.wait_ge(sums_scaled, n3 + 1)
                        dve.wait_ge(drop_raised, n3 + 1)
                        before = m.carried[(u3 - 1) % RING]
                        for k in range(4):
                            last = v.tensor_tensor_scan(m.carried[u3][:, k, :], drop[u3][:, k % 2, :], scaled[u3][:, k, :],
                                                        before[:, k, 127:128], ALU.mult, ALU.add)
                        last.then_inc(joined, 1)
                        dve.wait_ge(joined, n3 + 1)
                        at_least(dve, folded, n3 - 2)
                        v.reciprocal(ratio[u3][:, :, :], m.carried[u3][:, 0:2, :]).then_inc(inverted, 1)
                        dve.wait_ge(inverted, n3 + 1)
                        v.tensor_tensor(ratio[u3][:, :, :], ratio[u3][:, :, :], m.carried[u3][:, 2:4, :], ALU.mult).then_inc(ratio_ready, 1)
                steps(dve, step)


def norm_vector(v, eng, chain, t, spread_ready, root_ready):
    wide = [NP, NB, FEATS]
    chain(v.tensor_reduce(t.mean[:, :], t.x[:, :, :], X, ALU.add))
    chain(v.tensor_scalar(t.mean[:, :], t.mean[:, :], 1.0 / FEATS, None, ALU.mult))
    chain(v.tensor_tensor(t.x[:, :, :], t.x[:, :, :], t.mean[:, :].unsqueeze(2).broadcast_to(wide), ALU.subtract))
    chain(v.tensor_tensor(t.square[:, :, :], t.x[:, :, :], t.x[:, :, :], ALU.mult))
    chain(v.tensor_reduce(t.mean[:, :], t.square[:, :, :], X, ALU.add))
    v.tensor_scalar(t.mean[:, :], t.mean[:, :], 1.0 / FEATS, EPS, ALU.mult, ALU.add).then_inc(spread_ready, 1)
    eng.wait_ge(root_ready, 1)
    chain(v.reciprocal(t.root[:, :], t.root[:, :]))
    return v.tensor_tensor(t.out[:, :, :], t.x[:, :, :], t.root[:, :].unsqueeze(2).broadcast_to(wide), ALU.mult)


def finish_attention(nc, d, m, sem):
    ctx = ExitStack()
    with ctx:
        def sb(name, shape, dt=F32):
            return ctx.enter_context(nc.sbuf_tensor(name, shape, dt))

        node_sum = sb("node_sum", [NP, NB, FEATS])
        t = Tensors()
        t.x, t.out = m.node_x, m.node_x
        t.mean, t.root, t.square = sb("mean0", [NP, NB]), sb("root0", [NP, NB]), sb("square0", [NP, NB, FEATS])
        sums_in, spread_ready, root_ready, chain_sem = sem("node_sums_in"), sem("spread_ready0"), sem("root_ready0"), sem("norm0_chain")
        with nc.Block() as block:
            @block.gpsimd
            def _(pool):
                for b in range(NB):
                    pool.indirect_dma_start(node_sum[:, b, :], None, m.row_sums, bass.IndirectOffsetOnAxis(m.node_last[:, b:b + 1], 0)).then_inc(sums_in, 16)

            @block.scalar
            def _(act):
                act.wait_ge(spread_ready, 1)
                nc.scalar.activation(t.root[:, :], t.mean[:, :], ACT.Sqrt).then_inc(root_ready, 1)

            @block.vector
            def _(dve):
                chain = Chain(dve, chain_sem)
                v = nc.vector
                dve.wait_ge(sums_in, 16 * NB)
                chain(v.tensor_tensor(node_sum[:, :, :], node_sum[:, :, :], m.node_has[:, :].unsqueeze(2).broadcast_to([NP, NB, FEATS]), ALU.mult))
                chain(v.tensor_tensor(m.node_x[:, :, :], m.node_x[:, :, :], node_sum[:, :, :], ALU.add))
                chain(norm_vector(v, dve, chain, t, spread_ready, root_ready))


def segment_sums(nc, m, sem, values, width, table, tag, totals=None):
    ctx = ExitStack()
    with ctx:
        def sb(name, shape, dt=F32):
            return ctx.enter_context(nc.sbuf_tensor(f"{tag}_{name}", shape, dt))

        run = sb("run", [BLOCKS, 128, width])
        through = sb("through", [BLOCKS, 128])
        both = sb("both", [BLOCKS, 2, width])
        last_t = sb("last_t", [width, 2, BLOCKS])
        carry_t = sb("carry_t", [width, BLOCKS + 1])
        carry = sb("carry", [BLOCKS, width])
        chain_sem, turned, ends_ready, ends_turned = sem(f"{tag}_chain"), sem(f"{tag}_turned"), sem(f"{tag}_ends_ready"), sem(f"{tag}_ends_turned")
        carry_ready, carry_turned, run_ready, stored = sem(f"{tag}_carry_ready"), sem(f"{tag}_carry_turned"), sem(f"{tag}_run_ready"), sem(f"{tag}_stored")
        turned_ps = [m.psum[f // 4][0:BLOCKS, (f % 4) * 128:(f % 4 + 1) * 128] for f in range(width)]
        ends_ps = [m.psum[5 + i][0:width, 0:BLOCKS] for i in range(2)]
        carry_ps = m.psum[7][0:BLOCKS, 0:width]
        if totals is not None:
            after = sb("after", [BLOCKS, width, 128])
            back = sb("back", [BLOCKS, 128])
            heads = sb("heads", [BLOCKS, width])
            heads_t = sb("heads_t", [width, BLOCKS])
            next_t = sb("next_t", [width, BLOCKS + 1])
            heads_ready, heads_turned, next_ready, next_turned = (sem(f"{tag}_{x}") for x in ("heads_ready", "heads_turned", "next_ready", "next_turned"))
            whole_ready, whole_turned = sem(f"{tag}_whole_ready"), sem(f"{tag}_whole_turned")
            whole_ps = [m.psum[f // 4][:, (f % 4) * BLOCKS:(f % 4 + 1) * BLOCKS] for f in range(width)]

        with nc.Block() as block:
            @block.tensor
            def _(pe):
                t = nc.tensor
                for f in range(width):
                    last = t.transpose(turned_ps[f], values[:, f, :], m.ident[:, :])
                last.then_inc(turned, 1)
                pe.wait_ge(ends_ready, 1)
                for i in range(2):
                    last = t.transpose(ends_ps[i], both[:, i, :], m.ident[0:BLOCKS, 0:BLOCKS])
                last.then_inc(ends_turned, 1)
                pe.wait_ge(carry_ready, 1)
                t.transpose(carry_ps, carry_t[:, 0:BLOCKS], m.ident[0:width, 0:width]).then_inc(carry_turned, 1)
                if totals is not None:
                    pe.wait_ge(heads_ready, 1)
                    t.transpose(ends_ps[0], heads[:, :], m.ident[0:BLOCKS, 0:BLOCKS]).then_inc(heads_turned, 1)
                    pe.wait_ge(next_ready, 1)
                    t.transpose(carry_ps, next_t[:, 1:BLOCKS + 1], m.ident[0:width, 0:width]).then_inc(next_turned, 1)
                    pe.wait_ge(whole_ready, 1)
                    for f in range(width):
                        last = t.transpose(whole_ps[f], after[:, f, :], m.ident[0:BLOCKS, 0:BLOCKS])
                    last.then_inc(whole_turned, 1)

            @block.vector
            def _(dve):
                chain = Chain(dve, chain_sem)
                v = nc.vector
                keep = m.keep[:, 0:128]
                chain(v.tensor_tensor_scan(through[:, :], keep, keep, 1.0, ALU.mult, ALU.min))
                chain(v.tensor_copy(both[:, 1, :], through[:, 127:128].broadcast_to([BLOCKS, width])))
                dve.wait_ge(turned, 1)
                for f in range(width):
                    chain(v.tensor_tensor_scan(run[:, :, f], keep, turned_ps[f], 0.0, ALU.mult, ALU.add))
                v.tensor_copy(both[:, 0, :], run[:, 127, :]).then_inc(ends_ready, 1)
                dve.wait_ge(ends_turned, 1)
                for i in range(2):
                    chain(v.tensor_copy(last_t[:, i, :], ends_ps[i]))
                chain(v.memset(carry_t[:, 0:1], 0.0))
                v.tensor_tensor_scan(carry_t[:, 1:BLOCKS + 1], last_t[:, 1, :], last_t[:, 0, :], 0.0, ALU.mult, ALU.add).then_inc(carry_ready, 1)
                dve.wait_ge(carry_turned, 1)
                chain(v.tensor_copy(carry[:, :], carry_ps))
                for f in range(width):
                    last = v.scalar_tensor_tensor(run[:, :, f], through[:, :], carry[:, f:f + 1], run[:, :, f], ALU.mult, ALU.add)
                last.then_inc(run_ready, 1)
                if totals is None:
                    return
                dve.wait_ge(run_ready, 1)
                keep_next = m.keep[:, 1:129][:, ::-1]
                for f in range(width):
                    chain(v.tensor_tensor_scan(after[:, f, ::-1], keep_next, run[:, ::-1, f], 0.0, ALU.mult, ALU.max))
                chain(v.tensor_tensor_scan(back[:, ::-1], keep_next, keep_next, 1.0, ALU.mult, ALU.min))
                v.tensor_scalar(heads[:, :], after[:, :, 0], m.keep[:, 0:1], None, ALU.mult).then_inc(heads_ready, 1)
                dve.wait_ge(heads_turned, 1)
                chain(v.tensor_copy(heads_t[:, :], ends_ps[0]))
                chain(v.memset(next_t[:, BLOCKS:BLOCKS + 1], 0.0))
                v.tensor_tensor_scan(next_t[:, 0:BLOCKS][:, ::-1], last_t[:, 1, ::-1], heads_t[:, ::-1], 0.0, ALU.mult, ALU.max).then_inc(next_ready, 1)
                dve.wait_ge(next_turned, 1)
                chain(v.tensor_copy(carry[:, :], carry_ps))
                for f in range(width):
                    last = v.scalar_tensor_tensor(after[:, f, :], back[:, :], carry[:, f:f + 1], after[:, f, :], ALU.mult, ALU.max)
                last.then_inc(whole_ready, 1)
                dve.wait_ge(whole_turned, 1)
                for f in range(width):
                    last = v.tensor_copy(totals[:, f, :], whole_ps[f])
                chain(last)

            if totals is None:
                @block.sync
                def _(sp):
                    sp.wait_ge(run_ready, 1)
                    sp.dma_start(table.rearrange("(p r) f -> p r f", r=128), run[:, :, :]).then_inc(stored, 16)
                    sp.wait_ge(stored, 16)


def relation_norms(nc, d, m, sem):
    ctx = ExitStack()
    with ctx:
        def sb(name, shape, dt=F32):
            return ctx.enter_context(nc.sbuf_tensor(name, shape, dt))

        counts = sb("counts", [128, RELATIONS, BLOCKS])
        types = sb("types", [128, BLOCKS, SLOTS])
        match = sb("match", [128, BLOCKS, SLOTS])
        count_chain = sem("match_chain")
        whole = [128, BLOCKS, SLOTS]
        with nc.Block() as block:
            @block.vector
            def _(dve):
                chain = Chain(dve, count_chain)
                v = nc.vector
                chain(v.tensor_copy(types[:, :, :], m.edge_ids[:, :, :, 1]))
                chain(v.scalar_tensor_tensor(m.message_at[:, :, :], m.edge_ids[:, :, :, 0], float(RELATIONS), types[:, :, :], ALU.mult, ALU.add))
                for r in range(RELATIONS):
                    chain(v.scalar_tensor_tensor(match[:, :, :], types[:, :, :], float(r), m.used[:, :, :], ALU.is_equal, ALU.mult))
                    chain(v.tensor_reduce(counts[:, r, :], match[:, :, :], X, ALU.add))
        segment_sums(nc, m, sem, counts, RELATIONS, None, "count", totals=counts)
        norm_chain = sem("norm_chain")
        with nc.Block() as block:
            @block.vector
            def _(dve):
                chain = Chain(dve, norm_chain)
                v = nc.vector
                chain(v.tensor_scalar(counts[:, :, :], counts[:, :, :], 1.0, None, ALU.max))
                chain(v.reciprocal(counts[:, :, :], counts[:, :, :]))
                chain(v.memset(m.norm[:, :, :], 0.0))
                for r in range(RELATIONS):
                    chain(v.scalar_tensor_tensor(match[:, :, :], types[:, :, :], float(r), counts[:, r, :].unsqueeze(2).broadcast_to(whole), ALU.is_equal, ALU.mult))
                    chain(v.tensor_tensor(m.norm[:, :, :], m.norm[:, :, :], match[:, :, :], ALU.add))
                chain(v.tensor_tensor(m.norm[:, :, :], m.norm[:, :, :], m.used[:, :, :], ALU.mult))


def project(nc, d, m, sem, k):
    ctx = ExitStack()
    outs = RELATIONS * FEATS + FEATS
    x = m.node_x if k == 0 else m.hidden
    with ctx:
        def sb(name, shape, dt=F32):
            return ctx.enter_context(nc.sbuf_tensor(f"{name}{k}", shape, dt))

        x_t = sb("x_t", [FEATS + 1, NB, NP])
        weights = sb("layer_w", [FEATS + 1, outs])
        made = sb("made", [NP, NB, RELATIONS * FEATS])
        w_in, w_clear, ones_ready = sem(f"w_in{k}"), sem(f"w_clear{k}"), sem(f"ones_ready{k}")
        x_turned, x_ready, products, taken, table_out = sem(f"x_turned{k}"), sem(f"x_ready{k}"), sem(f"products{k}"), sem(f"taken{k}"), sem(f"table_out{k}")
        weights_in, root_in, bias_in = d.layers[k]
        GROUP = 3
        groups = [range(a, min(a + GROUP, NB)) for a in range(0, NB, GROUP)]
        with nc.Block() as block:
            @block.sync
            def _(sp):
                sp.wait_ge(w_clear, 1)
                sp.dma_start(weights[0:FEATS, 0:RELATIONS * FEATS].rearrange("i (r o) -> i r o", r=RELATIONS), weights_in.rearrange("r i o -> i r o")).then_inc(w_in, 16)
                sp.dma_start(weights[0:FEATS, RELATIONS * FEATS:], root_in).then_inc(w_in, 16)
                sp.dma_start(weights[FEATS:FEATS + 1, RELATIONS * FEATS:], bias_in.rearrange("(a n) -> a n", a=1)).then_inc(w_in, 16)
                sp.wait_ge(taken, len(groups))
                sp.dma_start(m.projected[k].rearrange("(p b r) o -> p b r o", b=NB, r=RELATIONS).rearrange("p b r o -> p (b r o)"),
                             made[:, :, :].rearrange("p b n -> p (b n)")).then_inc(table_out, 16)
                sp.wait_ge(table_out, 16)

            @block.gpsimd
            def _(pool):
                nc.gpsimd.memset(weights[:, :], 0.0).then_inc(w_clear, 1)
                nc.gpsimd.memset(x_t[:, :, :], 1.0).then_inc(ones_ready, 1)

            @block.tensor
            def _(pe):
                t = nc.tensor
                for b in range(NB):
                    if b >= 8:
                        pe.wait_ge(x_ready, b - 7)
                    t.transpose(m.psum[b % 8][0:FEATS, 0:NP], x[:, b, :], m.ident[0:NP, 0:NP]).then_inc(x_turned, 1)
                pe.wait_ge(w_in, 48)
                for n, group in enumerate(groups):
                    pe.wait_ge(x_ready, NB)
                    if n >= 8:
                        pe.wait_ge(taken, n - 7)
                    for i, b in enumerate(group):
                        last = t.matmul(m.psum[n % 8][0:NP, i * outs:(i + 1) * outs], x_t[:, b, :], weights[:, :], start=True, stop=True)
                    last.then_inc(products, 1)

            @block.vector
            def _(dve):
                v = nc.vector
                dve.wait_ge(ones_ready, 1)
                for b in range(NB):
                    dve.wait_ge(x_turned, b + 1)
                    v.tensor_copy(x_t[0:FEATS, b, :], m.psum[b % 8][0:FEATS, 0:NP]).then_inc(x_ready, 1)
                for n, group in enumerate(groups):
                    dve.wait_ge(products, n + 1)
                    bank = m.psum[n % 8][0:NP, 0:len(group) * outs].rearrange("p (b n) -> p b n", n=outs)
                    v.tensor_copy(m.rooted[:, group[0]:group[-1] + 1, :], bank[:, :, RELATIONS * FEATS:])
                    v.tensor_copy(made[:, group[0]:group[-1] + 1, :], bank[:, :, 0:RELATIONS * FEATS]).then_inc(taken, 1)


def gather_messages(nc, m, sem, sems, k):
    ctx = ExitStack()
    with ctx:
        def ring(name, shape, dt=F32):
            return [ctx.enter_context(nc.sbuf_tensor(f"{name}{k}_{u}", shape, dt)) for u in range(RING)]

        at = ring("at", [128, SLOTS], I32)
        got = ring("got", [128, SLOTS, FEATS])
        at_ready, got_in, weighted, reduced = sem(f"at_ready{k}"), [sem(f"got_in{k}_{u}") for u in range(RING)], sem(f"weighted{k}"), sem(f"reduced{k}")

        passed = sem(f"pool_passed{k}")

        def steps(eng, step):
            for u in range(RING):
                step(0, u)
            with eng.Fori(1, BLOCKS // RING) as q:
                for u in range(RING):
                    step(q, u)

        with nc.Block() as block:
            @block.gpsimd
            def _(pool):
                def step(q, u):
                    n = q * RING + u
                    at_least(pool, got_in[u], 16 * SLOTS * q)
                    nc.gpsimd.tensor_copy(at[u][:, :], m.message_at[:, bass.ds(n, 1), :].rearrange("p a s -> p (a s)")).then_inc(at_ready, 1)
                    pool.wait_ge(at_ready, n + 1)
                    at_least(pool, reduced, n - 2)
                    pool.sem_inc(passed, 1)
                    for s in range(SLOTS):
                        pool.indirect_dma_start(got[u][:, s, :], None, m.projected[k], bass.IndirectOffsetOnAxis(at[u][:, s:s + 1], 0)).then_inc(got_in[u], 16)
                steps(pool, step)

            @block.vector
            def _(dve):
                v = nc.vector

                def step(q, u):
                    n = q * RING + u
                    dve.wait_ge(got_in[u], 16 * SLOTS * (q + 1))
                    norm = m.norm[:, bass.ds(n, 1), :].rearrange("p a s -> p (a s)").unsqueeze(2).broadcast_to([128, SLOTS, FEATS])
                    v.tensor_tensor(got[u][:, :, :], got[u][:, :, :], norm, ALU.mult).then_inc(weighted, 1)
                    dve.wait_ge(weighted, n + 1)
                    v.tensor_reduce(m.messages[:, :, bass.ds(n, 1)].rearrange("p f a -> p (f a)"), got[u][:, :, :].rearrange("p s f -> p f s"), X, ALU.add).then_inc(reduced, 1)
                steps(dve, step)


def finish_layer(nc, d, m, sem, k, out):
    ctx = ExitStack()
    with ctx:
        def sb(name, shape, dt=F32):
            return ctx.enter_context(nc.sbuf_tensor(f"{name}_{k}", shape, dt))

        agg = sb("agg", [NP, NB, FEATS])
        top, power, total, result = sb("top", [NP, NB]), sb("power", [NP, NB, FEATS]), sb("total", [NP, NB]), sb("result", [NP, NB, FEATS])
        t = Tensors()
        t.x, t.out = agg, result
        t.mean, t.root, t.square = sb("mean", [NP, NB]), sb("root", [NP, NB]), sb("square", [NP, NB, FEATS])
        aggs_in, chain_sem = sem(f"aggs_in{k}"), sem(f"finish_chain{k}")
        shifted, raised, totals_ready, logs_ready = sem(f"z_shifted{k}"), sem(f"z_raised{k}"), sem(f"z_totals{k}"), sem(f"z_logs{k}")
        spread_ready, root_ready, result_ready, stored = sem(f"z_spread{k}"), sem(f"z_root{k}"), sem(f"z_result{k}"), sem(f"z_stored{k}")
        wide = [NP, NB, FEATS]
        with nc.Block() as block:
            @block.gpsimd
            def _(pool):
                for b in range(NB):
                    pool.indirect_dma_start(agg[:, b, :], None, m.row_aggs[k], bass.IndirectOffsetOnAxis(m.node_last[:, b:b + 1], 0)).then_inc(aggs_in, 16)

            if k == 1:
                @block.scalar
                def _(act):
                    act.wait_ge(shifted, 1)
                    nc.scalar.activation(power[:, :, :], agg[:, :, :], ACT.Exp).then_inc(raised, 1)
                    act.wait_ge(totals_ready, 1)
                    nc.scalar.activation(total[:, :], total[:, :], ACT.Ln).then_inc(logs_ready, 1)
                    act.wait_ge(spread_ready, 1)
                    nc.scalar.activation(t.root[:, :], t.mean[:, :], ACT.Sqrt).then_inc(root_ready, 1)

                @block.sync
                def _(sp):
                    sp.wait_ge(result_ready, 1)
                    sp.dma_start(out.rearrange("(p b) f -> p b f", b=NB), result[:, :, :]).then_inc(stored, 16)
                    sp.wait_ge(stored, 16)

            @block.vector
            def _(dve):
                chain = Chain(dve, chain_sem)
                v = nc.vector
                dve.wait_ge(aggs_in, 16 * NB)
                chain(v.tensor_tensor(agg[:, :, :], agg[:, :, :], m.node_has[:, :].unsqueeze(2).broadcast_to(wide), ALU.mult))
                chain(v.tensor_tensor(agg[:, :, :], agg[:, :, :], m.rooted[:, :, :], ALU.add))
                if k == 0:
                    chain(v.tensor_scalar(m.hidden[:, :, :], agg[:, :, :], 0.0, None, ALU.max))
                    return
                chain(v.tensor_reduce(top[:, :], agg[:, :, :], X, ALU.max))
                v.tensor_tensor(agg[:, :, :], agg[:, :, :], top[:, :].unsqueeze(2).broadcast_to(wide), ALU.subtract).then_inc(shifted, 1)
                dve.wait_ge(raised, 1)
                v.tensor_reduce(total[:, :], power[:, :, :], X, ALU.add).then_inc(totals_ready, 1)
                dve.wait_ge(logs_ready, 1)
                chain(v.tensor_tensor(agg[:, :, :], agg[:, :, :], total[:, :].unsqueeze(2).broadcast_to(wide), ALU.subtract))
                chain(v.tensor_tensor(agg[:, :, :], agg[:, :, :], m.node_x[:, :, :], ALU.add))
                norm_vector(v, dve, chain, t, spread_ready, root_ready).then_inc(result_ready, 1)


def kernel(x, src, dst, edge_attr_16, edge_type_8, L0_gnn_W_msg, L0_gnn_b_msg, L0_gnn_W_attn, L0_gnn_b_attn,
           L1_gnn_W1, L1_gnn_root1, L1_gnn_b1, L1_gnn_W2, L1_gnn_root2, L1_gnn_b2):
    import numpy as np
    import concourse.bacc as bacc
    from concourse.bass_utils import run_bass_kernel_spmd as run

    efeat = np.zeros((EDGES + SLOTS, FEATS), np.float32)
    efeat[0:EDGES] = edge_attr_16
    ids = np.zeros((EDGES + SLOTS, 2), np.int32)
    ids[0:EDGES, 0] = src
    ids[0:EDGES, 1] = edge_type_8
    arrays = {
        "x": x, "dst": dst, "efeat": efeat, "ids": ids,
        "w_msg": L0_gnn_W_msg, "b_msg": L0_gnn_b_msg, "w_attn": L0_gnn_W_attn, "b_attn": L0_gnn_b_attn,
        "w1": L1_gnn_W1, "root1": L1_gnn_root1, "b1": L1_gnn_b1, "w2": L1_gnn_W2, "root2": L1_gnn_root2, "b2": L1_gnn_b2,
    }
    arrays = {f"in_{name}": np.ascontiguousarray(a) for name, a in arrays.items()}
    nc = bacc.Bacc("TRN2", target_bir_lowering=False, num_devices=1)
    given = {name[3:]: nc.dram_tensor(name, a.shape, mybir.dt.from_np(a.dtype), kind="ExternalInput").ap() for name, a in arrays.items()}
    d = Tensors()
    d.x, d.dst, d.efeat, d.ids = given["x"], given["dst"], given["efeat"], given["ids"]
    d.w_msg, d.b_msg, d.w_attn, d.b_attn = given["w_msg"], given["b_msg"], given["w_attn"], given["b_attn"]
    d.layers = [(given["w1"], given["root1"], given["b1"]), (given["w2"], given["root2"], given["b2"])]
    out = nc.dram_tensor("out", (NODES, FEATS), F32, kind="ExternalOutput").ap()
    build(nc, d, out)
    return run(nc, [arrays], core_ids=[0]).results[0]["out"]
```

```python
import concourse.bass as bass
from concourse import mybir
from contextlib import ExitStack

F32 = mybir.dt.float32
F16 = mybir.dt.float16
BF16 = mybir.dt.bfloat16
I32 = mybir.dt.int32
ALU = mybir.AluOpType
ACT = mybir.ActivationFunctionType
X = mybir.AxisListType.X

NODES = 3125
EDGES = 103125
FEATS = 16
RELATIONS = 8
CHANNELS = FEATS * FEATS
EPS = 1e-5

SLOTS = 8
BLOCKS = -(-((EDGES + NODES * (SLOTS - 1)) // SLOTS) // 128)
RING = 3
BLOCKS += -BLOCKS % RING
ROWS = BLOCKS * 128
RUN = SLOTS * FEATS
ACT_SLOTS = (0,)
VEC_SLOTS = tuple(s for s in range(SLOTS) if s not in ACT_SLOTS)

NP, NB = 125, 25
CUTS, CUT = 275, 375
PIECES = 6
CODED = PIECES * FEATS + 3

TABLE_AT, MATRIX_AT = (0, 3, 5, 8), (1, 2, 4, 6, 7, 9)
TABLE_AFTER = (1, 2, 4, 5)
TABLE_TURNS, MATRIX_TURNS = len(TABLE_AT), len(MATRIX_AT)
TURNS = TABLE_TURNS + MATRIX_TURNS
LAPS = -(-BLOCKS // TURNS)
LEFT = BLOCKS - TURNS * (LAPS - 1)
LINES = 5
ACT_LINES = (3, 4)
VEC_LINES = (0, 1, 2)
WITHIN = LINES * 128
PAGES = -(-NODES // WITHIN)

LOWEST = -1e37
OFF = -1e30


class Tensors:
    pass


class Chain:

    def __init__(self, eng, sem):
        self.eng, self.sem, self.n = eng, sem, 0

    def __call__(self, instruction):
        instruction.then_inc(self.sem, 1)
        self.n += 1
        self.eng.wait_ge(self.sem, self.n)


def at_least(eng, sem, value):
    if not isinstance(value, int) or value > 0:
        eng.wait_ge(sem, value)




def build(nc, d, out):
    ctx = ExitStack()
    with ctx:
        def sb(name, shape, dt=F32):
            return ctx.enter_context(nc.sbuf_tensor(name, shape, dt))

        in_use = []

        def sem(name):
            in_use.append(nc.alloc_semaphore(name=name))
            return in_use[-1]

        def sems(name):
            return [sem(f"{name}{u}") for u in range(RING)]

        def phase_ends():
            nc.all_engine_barrier()
            nc.clear_and_free_semaphores(in_use)
            in_use.clear()
            nc.all_engine_barrier()

        m = Tensors()
        m.row_table = nc.dram_tensor("row_table", (ROWS, 4), F32, kind="Internal").ap()
        m.restart_table = nc.dram_tensor("restart_table", (ROWS,), F32, kind="Internal").ap()
        m.row_sums = nc.dram_tensor("row_sums", (ROWS, 4 * 128), F32, kind="Internal").ap()
        m.within_table = nc.dram_tensor("within_table", (BLOCKS * SLOTS, 128), F16, kind="Internal").ap()
        m.node_table = [nc.dram_tensor(f"node_table{k}", (NODES, FEATS), F32, kind="Internal").ap() for k in range(2)]
        m.projected = [nc.dram_tensor(f"projected{k}", (NODES * RELATIONS, FEATS), F32, kind="Internal").ap() for k in range(2)]
        m.row_aggs = [nc.dram_tensor(f"row_aggs{k}", (ROWS, FEATS), F32, kind="Internal").ap() for k in range(2)]
        m.ident = sb("ident", [128, 128])
        m.ident16 = sb("ident16", [128, 128], BF16)
        m.ones_row = sb("ones_row", [1, 128])
        m.slot_no = sb("slot_no", [128, SLOTS])
        m.facts = sb("facts", [128, BLOCKS, 1 + SLOTS], I32)
        m.used = sb("used", [128, BLOCKS, SLOTS])
        m.off = sb("off", [128, BLOCKS, SLOTS])
        m.keep = sb("keep", [BLOCKS, 129])
        m.node_last = sb("node_last", [NP, NB], I32)
        m.node_has = sb("node_has", [NP, NB])
        m.edge_ids = sb("edge_ids", [128, BLOCKS, SLOTS, 2], I32)
        m.coded_w = sb("coded_w", [CODED, 2 * CHANNELS], BF16)
        m.node_x = sb("node_x", [NP, NB, FEATS])
        m.norm = sb("norm", [128, BLOCKS, SLOTS])
        m.typed_norm = sb("typed_norm", [128, BLOCKS, SLOTS, RELATIONS])
        m.page = sb("page", [128, BLOCKS, SLOTS])
        m.page_no = sb("page_no", [128, PAGES])
        m.line_no = sb("line_no", [128, LINES])
        m.minus_line = sb("minus_line", [128, LINES])
        m.x_parts = sb("x_parts", [128, 3, LINES, PAGES * FEATS], BF16)
        m.stacked_w = sb("stacked_w", [128, FEATS])
        m.message_at = sb("message_at", [128, BLOCKS, SLOTS], I32)
        m.messages = sb("messages", [128, FEATS, BLOCKS])
        m.hidden = sb("hidden", [NP, NB, FEATS])
        m.rooted = sb("rooted", [NP, NB, FEATS])
        m.psum = [ctx.enter_context(nc.psum_tensor(f"bank{i}", [128, 512], F32)) for i in range(8)]
        m.coded = [sb(f"coded{u}", [128, SLOTS, CODED], BF16) for u in range(RING)]
        m.peak = [sb(f"run_peak{u}", [128, 2, 129]) for u in range(RING)]
        m.carried = [sb(f"carried{u}", [128, 4, 128]) for u in range(RING)]

        make_rows(nc, d, m, sem)
        phase_ends()
        attention(nc, d, m, sem, sems)
        phase_ends()
        with ExitStack() as m.ctx:
            l = last_sums(nc, m, sem)
            relation_norms(nc, d, m, sem, l)
            finish_attention(nc, d, m, sem, l)
        for k in range(2):
            phase_ends()
            project(nc, d, m, sem, k)
            gather_messages(nc, m, sem, sems, k)
            segment_sums(nc, m, sem, m.messages, FEATS, m.row_aggs[k], f"agg{k}")
            finish_layer(nc, d, m, sem, k, out)


def make_rows(nc, d, m, sem):
    ctx = ExitStack()
    with ctx:
        def sb(name, shape, dt=F32):
            return ctx.enter_context(nc.sbuf_tensor(name, shape, dt))

        heads_i = sb("heads_i", [1, CUTS], I32)
        heads = sb("heads", [1, CUTS])
        node_i = sb("node_i", [NP, NB + 1], I32)
        node_no = sb("node_no", [NP, NB + 1])
        before = sb("before", [NP, NB + 1, CUT])
        piece = sb("piece", [NP, NB + 1, CUT], I32)
        cut_no = sb("cut_no", [NP, NB + 1])
        cut_i = sb("cut_i", [NP, NB + 1], I32)
        inside = sb("inside", [NP, NB + 1])
        start = sb("start", [NP, NB + 1])
        upto_i = sb("upto_i", [NP, NB], I32)
        count = sb("count", [NP, NB])
        last = sb("last", [NP, NB])
        base = sb("base", [NP, 1])
        ones = sb("ones", [NP, NB])
        earlier = sb("earlier", [NP, NP])
        to_row = sb("to_row", [NP, NB])
        to_row_i = sb("to_row_i", [NP, NB], I32)
        entry = sb("entry", [NP, NB, 4])
        zeros = sb("zeros", [BLOCKS, 512])
        table = sb("table", [BLOCKS, 128, 4])
        filled = sb("filled", [BLOCKS, 4, 128])
        ends = sb("ends", [BLOCKS, 4])
        carry_t = sb("carry_t", [4, BLOCKS + 1])
        carry = sb("carry", [BLOCKS, 4])
        row_i = sb("row_i", [BLOCKS, 128], I32)
        row_no = sb("row_no", [BLOCKS, 128])
        first = sb("first", [BLOCKS, 128])
        begin = sb("begin", [BLOCKS, 128])
        length = sb("length", [BLOCKS, 128])
        restart = sb("restart", [BLOCKS, 128])
        length_t = sb("length_t", [128, BLOCKS])
        slot_i = sb("slot_i", [128, SLOTS], I32)
        w_in = sb("w_in", [FEATS, 2 * CHANNELS])
        b_in = sb("b_in", [1, 2 * CHANNELS])
        w_rest = sb("w_rest", [FEATS, 2 * CHANNELS])
        b_rest = sb("b_rest", [1, 2 * CHANNELS])
        w_parts = sb("w_parts", [FEATS, 3, 2 * CHANNELS], BF16)
        b_parts = sb("b_parts", [1, 3, 2 * CHANNELS], BF16)

        heads_in, weights_in, table_clear, x_in = sem("heads_in"), sem("weights_in"), sem("table_clear"), sem("x_in")
        table_in, restart_out, coded_w_in = sem("table_in"), sem("restart_out"), sem("coded_w_in")
        pool_chain, vec_chain = sem("rows_pool_chain"), sem("rows_vec_chain")
        constants, heads_ready, heads_spread = sem("constants"), sem("heads_ready"), sem("heads_spread")
        cuts_ready, pieces_in, totals_ready, bases_ready = sem("cuts_ready"), sem("pieces_in"), sem("totals_ready"), sem("bases_ready")
        entries_ready, entries_out, zeros_ready = sem("entries_ready"), sem("entries_out"), sem("zeros_ready")
        ends_ready, ends_turned, carry_ready, carry_turned = sem("ends_ready"), sem("ends_turned"), sem("carry_ready"), sem("carry_turned")
        rows_ready, rows_turned, parts_ready = sem("rows_ready"), sem("rows_turned"), sem("parts_ready")

        heads_ps, base_ps = m.psum[0][0:NP, 0:CUTS], m.psum[1][0:NP, 0:1]
        ends_ps, carry_ps = m.psum[2][0:4, 0:BLOCKS], m.psum[3][0:BLOCKS, 0:4]
        begin_ps, length_ps = m.psum[4][:, 0:BLOCKS], m.psum[5][:, 0:BLOCKS]

        with nc.Block() as block:
            @block.sync
            def _(sp):
                with nc.allow_non_contiguous_dma(reason="one destination in each piece"):
                    sp.dma_start(heads_i[:, :], d.dst.rearrange("(a c) -> a c", c=CUT)[:, 0:1].rearrange("a c -> c a")).then_inc(heads_in, 16)
                sp.dma_start(w_in[:, 0:CHANNELS], d.w_attn).then_inc(weights_in, 16)
                sp.dma_start(w_in[:, CHANNELS:], d.w_msg).then_inc(weights_in, 16)
                sp.dma_start(b_in[:, 0:CHANNELS], d.b_attn.rearrange("(a n) -> a n", a=1)).then_inc(weights_in, 16)
                sp.dma_start(b_in[:, CHANNELS:], d.b_msg.rearrange("(a n) -> a n", a=1)).then_inc(weights_in, 16)
                sp.dma_start(m.node_x[:, :, :], d.x.rearrange("(p b) f -> p b f", b=NB)).then_inc(x_in, 16)
                sp.wait_ge(zeros_ready, 1)
                sp.dma_start(m.row_table.rearrange("(p r) c -> p (r c)", r=128), zeros[:, :]).then_inc(table_clear, 16)
                sp.wait_ge(parts_ready, 1)
                for row, part in enumerate((0, 1, 2, 0, 1, 0)):
                    sp.dma_start(m.coded_w[row * FEATS:(row + 1) * FEATS, :], w_parts[:, part, :]).then_inc(coded_w_in, 16)
                for part in range(3):
                    sp.dma_start(m.coded_w[PIECES * FEATS + part:PIECES * FEATS + part + 1, :], b_parts[:, part, :]).then_inc(coded_w_in, 16)
                sp.wait_ge(entries_out, 16 * NB)
                sp.dma_start(table[:, :, :], m.row_table.rearrange("(p r) c -> p r c", r=128)).then_inc(table_in, 16)
                sp.wait_ge(rows_ready, 1)
                sp.dma_start(m.restart_table.rearrange("(p r) -> p r", r=128), restart[:, :]).then_inc(restart_out, 16)
                sp.wait_ge(restart_out, 16)
                sp.wait_ge(coded_w_in, 16 * (PIECES + 3))
                sp.wait_ge(x_in, 16)

            @block.gpsimd
            def _(pool):
                chain = Chain(pool, pool_chain)
                nc.gpsimd.memset(zeros[:, :], 0.0).then_inc(zeros_ready, 1)
                chain(nc.gpsimd.iota(node_i[:, :], pattern=[[1, NB + 1]], base=0, channel_multiplier=NB))
                chain(nc.gpsimd.iota(row_i[:, :], pattern=[[1, 128]], base=0, channel_multiplier=128))
                chain(nc.gpsimd.iota(slot_i[:, :], pattern=[[1, SLOTS]], base=0, channel_multiplier=0))
                chain(nc.gpsimd.memset(m.ident[:, :], 0.0))
                chain(nc.gpsimd.memset(m.ones_row[:, :], 1.0))
                chain(nc.gpsimd.memset(ones[:, :], 1.0))
                chain(nc.gpsimd.memset(earlier[:, :], 1.0))
                chain(nc.gpsimd.affine_select(out=m.ident[:, :], in_=m.ident[:, :], compare_op=ALU.not_equal, fill=1.0,
                                              base=0, pattern=[[-1, 128]], channel_multiplier=1))
                chain(nc.gpsimd.affine_select(out=earlier[:, :], in_=earlier[:, :], compare_op=ALU.is_gt, fill=0.0,
                                              base=0, pattern=[[1, NP]], channel_multiplier=-1))
                for u in range(RING):
                    chain(nc.gpsimd.memset(m.coded[u][:, :, PIECES * FEATS:CODED], 1.0))
                chain(nc.gpsimd.memset(m.peak[RING - 1][:, :, 128:129], LOWEST))
                chain(nc.gpsimd.memset(m.carried[RING - 1][:, :, :], 0.0))
                nc.gpsimd.memset(m.keep[:, 128:129], 1.0).then_inc(constants, 1)
                pool.wait_ge(cuts_ready, 1)
                for b in range(NB + 1):
                    pool.indirect_dma_start(piece[:, b, :], None, d.dst.rearrange("(a c) -> a c", c=CUT),
                                            bass.IndirectOffsetOnAxis(cut_i[:, b:b + 1], 0)).then_inc(pieces_in, 16)
                pool.wait_ge(entries_ready, 1)
                pool.wait_ge(table_clear, 16)
                for b in range(NB):
                    pool.indirect_dma_start(m.row_table, bass.IndirectOffsetOnAxis(to_row_i[:, b:b + 1], 0), entry[:, b, :], None,
                                            bounds_check=ROWS - 1, oob_is_err=False).then_inc(entries_out, 16)
                pool.wait_ge(entries_out, 16 * NB)

            @block.tensor
            def _(pe):
                pe.wait_ge(constants, 1)
                pe.wait_ge(heads_ready, 1)
                nc.tensor.matmul(heads_ps, m.ones_row[:, 0:NP], heads[:, :], start=True, stop=True).then_inc(heads_spread, 1)
                pe.wait_ge(totals_ready, 1)
                nc.tensor.matmul(base_ps, earlier[:, :], last[:, NB - 1:NB], start=True, stop=True).then_inc(bases_ready, 1)
                pe.wait_ge(ends_ready, 1)
                nc.tensor.transpose(ends_ps, ends[:, :], m.ident[0:BLOCKS, 0:BLOCKS]).then_inc(ends_turned, 1)
                pe.wait_ge(carry_ready, 1)
                nc.tensor.transpose(carry_ps, carry_t[:, 0:BLOCKS], m.ident[0:4, 0:4]).then_inc(carry_turned, 1)
                pe.wait_ge(rows_ready, 1)
                nc.tensor.transpose(begin_ps, begin[:, :], m.ident[0:BLOCKS, 0:BLOCKS]).then_inc(rows_turned, 1)
                nc.tensor.transpose(length_ps, length[:, :], m.ident[0:BLOCKS, 0:BLOCKS]).then_inc(rows_turned, 1)

            @block.vector
            def _(dve):
                chain = Chain(dve, vec_chain)
                v = nc.vector
                dve.wait_ge(heads_in, 16)
                v.tensor_copy(heads[:, :], heads_i[:, :]).then_inc(heads_ready, 1)
                dve.wait_ge(constants, 1)
                chain(v.tensor_copy(node_no[:, :], node_i[:, :]))
                chain(v.tensor_copy(row_no[:, :], row_i[:, :]))
                chain(v.tensor_copy(m.slot_no[:, :], slot_i[:, :]))
                chain(v.tensor_copy(m.ident16[:, :], m.ident[:, :]))
                dve.wait_ge(heads_spread, 1)
                chain(v.tensor_tensor(before[:, :, 0:CUTS], heads_ps.unsqueeze(1).broadcast_to([NP, NB + 1, CUTS]),
                                      node_no[:, :].unsqueeze(2).broadcast_to([NP, NB + 1, CUTS]), ALU.is_lt))
                chain(v.tensor_reduce(cut_no[:, :], before[:, :, 0:CUTS], X, ALU.add))
                chain(v.tensor_scalar(cut_no[:, :], cut_no[:, :], -1.0, 0.0, ALU.add, ALU.max))
                v.tensor_copy(cut_i[:, :], cut_no[:, :]).then_inc(cuts_ready, 1)
                dve.wait_ge(weights_in, 64)
                for whole, rest, parts in ((w_in, w_rest, w_parts), (b_in, b_rest, b_parts)):
                    chain(v.tensor_copy(parts[:, 0, :], whole[:, :]))
                    chain(v.tensor_tensor(rest[:, :], whole[:, :], parts[:, 0, :], ALU.subtract))
                    chain(v.tensor_copy(parts[:, 1, :], rest[:, :]))
                    chain(v.tensor_tensor(rest[:, :], rest[:, :], parts[:, 1, :], ALU.subtract))
                    if parts is w_parts:
                        chain(v.tensor_copy(parts[:, 2, :], rest[:, :]))
                v.tensor_copy(b_parts[:, 2, :], b_rest[:, :]).then_inc(parts_ready, 1)
                dve.wait_ge(pieces_in, 16 * (NB + 1))
                chain(v.tensor_tensor(before[:, :, :], piece[:, :, :], node_no[:, :].unsqueeze(2).broadcast_to([NP, NB + 1, CUT]), ALU.is_lt))
                chain(v.tensor_reduce(inside[:, :], before[:, :, :], X, ALU.add))
                chain(v.scalar_tensor_tensor(start[:, :], cut_no[:, :], float(CUT), inside[:, :], ALU.mult, ALU.add))
                chain(v.tensor_tensor(count[:, :], start[:, 1:NB + 1], start[:, 0:NB], ALU.subtract))
                chain(v.tensor_scalar(upto_i[:, :], count[:, :], float(SLOTS - 1), None, ALU.add))
                chain(v.tensor_scalar(upto_i[:, :], upto_i[:, :], SLOTS.bit_length() - 1, None, ALU.arith_shift_right))
                chain(v.tensor_copy(count[:, :], upto_i[:, :]))
                v.tensor_tensor_scan(last[:, :], ones[:, :], count[:, :], 0.0, ALU.mult, ALU.add).then_inc(totals_ready, 1)
                dve.wait_ge(bases_ready, 1)
                chain(v.tensor_copy(base[:, :], base_ps))
                chain(v.tensor_scalar(last[:, :], last[:, :], base[:, :], None, ALU.add))
                chain(v.tensor_scalar(m.node_has[:, :], count[:, :], 0.0, None, ALU.is_gt))
                chain(v.tensor_copy(entry[:, :, 0], start[:, 0:NB]))
                chain(v.tensor_copy(entry[:, :, 1], start[:, 1:NB + 1]))
                chain(v.tensor_tensor(entry[:, :, 2], last[:, :], count[:, :], ALU.subtract))
                chain(v.tensor_scalar(entry[:, :, 3], node_no[:, 0:NB], 1.0, None, ALU.add))
                chain(v.tensor_scalar(to_row[:, :], m.node_has[:, :], -2.0 * ROWS, 2.0 * ROWS, ALU.mult, ALU.add))
                chain(v.tensor_tensor(to_row[:, :], to_row[:, :], entry[:, :, 2], ALU.add))
                chain(v.tensor_copy(to_row_i[:, :], to_row[:, :]))
                chain(v.tensor_scalar(last[:, :], last[:, :], -1.0, 0.0, ALU.add, ALU.max))
                v.tensor_copy(m.node_last[:, :], last[:, :]).then_inc(entries_ready, 1)
                dve.wait_ge(table_in, 16)
                for c in range(4):
                    chain(v.tensor_tensor_scan(filled[:, c, :], table[:, :, c], table[:, :, c], 0.0, ALU.max, ALU.max))
                chain(v.memset(carry_t[:, 0:1], 0.0))
                v.tensor_copy(ends[:, :], filled[:, :, 127]).then_inc(ends_ready, 1)
                dve.wait_ge(ends_turned, 1)
                chain(v.tensor_copy(carry_t[:, 1:BLOCKS + 1], ends_ps))
                v.tensor_tensor_scan(carry_t[:, 1:BLOCKS + 1], carry_t[:, 1:BLOCKS + 1], carry_t[:, 1:BLOCKS + 1], 0.0,
                                     ALU.max, ALU.max).then_inc(carry_ready, 1)
                dve.wait_ge(carry_turned, 1)
                chain(v.tensor_copy(carry[:, :], carry_ps))
                for c in range(3):
                    chain(v.tensor_scalar(filled[:, c, :], filled[:, c, :], carry[:, c:c + 1], None, ALU.max))
                chain(v.tensor_tensor(row_no[:, :], row_no[:, :], filled[:, 2, :], ALU.subtract))
                chain(v.scalar_tensor_tensor(begin[:, :], row_no[:, :], float(SLOTS), filled[:, 0, :], ALU.mult, ALU.add))
                chain(v.tensor_scalar(begin[:, :], begin[:, :], float(EDGES), None, ALU.min))
                chain(v.tensor_tensor(length[:, :], filled[:, 1, :], begin[:, :], ALU.subtract))
                chain(v.tensor_scalar(first[:, :], table[:, :, 3], 0.0, None, ALU.is_gt))
                chain(v.tensor_scalar(m.keep[:, 0:128], first[:, :], -1.0, 1.0, ALU.mult, ALU.add))
                v.tensor_scalar(restart[:, :], first[:, :], LOWEST, None, ALU.mult).then_inc(rows_ready, 1)
                dve.wait_ge(rows_turned, 2)
                chain(v.tensor_copy(m.facts[:, :, 0], begin_ps))
                chain(v.tensor_copy(length_t[:, :], length_ps))
                chain(v.tensor_tensor(m.used[:, :, :], m.slot_no[:, :].unsqueeze(1).broadcast_to([128, BLOCKS, SLOTS]),
                                      length_t[:, :].unsqueeze(2).broadcast_to([128, BLOCKS, SLOTS]), ALU.is_lt))
                chain(v.tensor_scalar(m.facts[:, :, 1:1 + SLOTS], m.used[:, :, :], -1.0, 1.0, ALU.mult, ALU.add))
                chain(v.tensor_scalar(m.off[:, :, :], m.used[:, :, :], -OFF, OFF, ALU.mult, ALU.add))


def attention(nc, d, m, sem, sems):
    ctx = ExitStack()
    with ctx:
        def ring(name, shape, dt=F32):
            return [ctx.enter_context(nc.sbuf_tensor(f"{name}{u}", shape, dt)) for u in range(RING)]

        facts = ring("facts_at", [128, 1 + SLOTS], I32)
        ids = ring("ids", [128, SLOTS, 2], I32)
        feats = ring("feats", [128, SLOTS, FEATS])
        rest = ring("rest", [128, SLOTS, FEATS])
        sources = ring("sources", [128, SLOTS, FEATS])
        turned = ring("turned_feats", [CODED, SLOTS, 128], BF16)
        pair = ring("pair", [128, SLOTS, 2, CHANNELS])
        row_peak = ring("row_peak", [128, CHANNELS])
        sums = ring("sums", [128, 2 * CHANNELS])
        restart = ring("restart_at", [128, 128])
        below = ring("below", [128, 2, 128])
        drop = ring("drop", [128, 2, 128])
        scaled = ring("scaled", [128, 4, 128])
        stored = ring("stored", [128, 4, 128])

        vec_ps, act_ps = m.psum[0:2], m.psum[2]
        back_ps = m.psum[3][:, :].rearrange("p (k c) -> p k c", k=4)
        turn_ps = m.psum[4][0:CODED, :].bitcast(BF16).rearrange("p (s r) -> p s r", s=SLOTS)
        sums_ps = m.psum[5]
        sums_t_ps = m.psum[6][:, :].rearrange("p (k r) -> p k r", k=4)
        peak_t_ps = m.psum[7][:, 0:256].rearrange("p (k r) -> p k r", k=2)

        facts_ready, runs_in, picked, kept = sem("facts_ready"), sems("runs_in"), sem("picked"), sem("kept")
        sources_in, high_ready, high_off = sems("sources_in"), sem("high_ready"), sem("high_off")
        mid_ready, mid_off, low_ready = sem("mid_ready"), sem("mid_off"), sem("low_ready")
        feats_turned, feats_ready, weights_made = sem("feats_turned"), sem("feats_ready"), sem("weights_made")
        vec_made, act_made, row_peaked, shifted, raised = sem("vec_made"), sem("act_made"), sem("row_peaked"), sem("shifted"), sem("raised")
        weighed, summed, sums_ready, sums_turned = sem("weighed"), sem("summed"), sem("sums_ready"), sem("sums_turned")
        restart_in, peak_run, below_ready, restarted = sems("restart_in"), sem("peak_run"), sem("below_ready"), sem("restarted")
        drop_ready, below_raised, drop_raised = sem("drop_ready"), sem("below_raised"), sem("drop_raised")
        sums_scaled, joined = sem("sums_scaled"), sem("joined")
        pool_passed, dve_passed = sem("pool_passed"), sem("dve_passed")
        joined_turned, out_ready, out_stored = sem("joined_turned"), sem("out_ready"), sems("out_stored")

        def shifted_by(q, u, by):
            w = u + by
            q, u = q + w // RING, w % RING
            return q, u, q * RING + u

        def is_block(n):
            return not isinstance(n, int) or 0 <= n < BLOCKS

        LOOP = (2, (BLOCKS - 3) // RING)

        def steps(eng, step):
            for n in range(-RING, RING * LOOP[0]):
                step(n // RING, n % RING)
            with eng.Fori(*LOOP) as q:
                for u in range(RING):
                    step(q, u)
            for n in range(RING * LOOP[1], BLOCKS + 4):
                step(n // RING, n % RING)

        with nc.Block() as block:
            @block.sync
            def _(sp):
                def step(q, u):
                    q3, u3, n3 = shifted_by(q, u, -2)
                    if is_block(n3):
                        at_least(sp, drop_ready, n3 - 2)
                        sp.dma_start(restart[u3][:, :], m.restart_table[bass.ds(n3 * 128, 128)].partition_broadcast(128)).then_inc(restart_in[u3], 16)
                    q4, u4, n4 = shifted_by(q, u, -4)
                    if is_block(n4):
                        sp.wait_ge(out_ready, n4 + 1)
                        sp.dma_start(m.row_sums[bass.ds(n4 * 128, 128), :], stored[u4][:, :, :].rearrange("p k c -> p (k c)")).then_inc(out_stored[u4], 16)
                steps(sp, step)
                for u in range(RING):
                    sp.wait_ge(out_stored[u], 16 * (BLOCKS // RING))

            @block.gpsimd
            def _(pool):
                g = nc.gpsimd

                def step(q, u):
                    q1, u1, n1 = shifted_by(q, u, 1)
                    q2, u2, n2 = shifted_by(q, u, 2)
                    q3, u3, n3 = shifted_by(q, u, -3)
                    qa, ua, na = shifted_by(q, u, 3)

                    def gather(slots):
                        for s in slots:
                            pool.indirect_dma_start(sources[u1][:, s, :], None, d.x, bass.IndirectOffsetOnAxis(ids[u1][:, s, 0:1], 0)).then_inc(sources_in[u1], 16)

                    if is_block(n1):
                        pool.wait_ge(picked, 2 * n1 + 2)
                        at_least(pool, vec_made, len(VEC_SLOTS) * (n1 - 2))
                        at_least(pool, act_made, len(ACT_SLOTS) * (n1 - 2))
                        pool.sem_inc(pool_passed, 1)
                        gather(range(0, SLOTS // 2))
                    if is_block(n3):
                        pool.wait_ge(peak_run, 3 * n3 + 3)
                        pool.wait_ge(restart_in[u3], 16 * q3 + 16)
                        at_least(pool, joined, n3 - 2)
                        g.tensor_tensor(drop[u3][:, :, :], m.peak[u3][:, :, 0:128],
                                        restart[u3][:, :].unsqueeze(1).broadcast_to([128, 2, 128]), ALU.add).then_inc(restarted, 1)
                        pool.wait_ge(restarted, n3 + 1)
                        g.tensor_tensor(drop[u3][:, :, :], drop[u3][:, :, :], m.peak[u3][:, :, 1:129], ALU.subtract).then_inc(drop_ready, 1)
                    if is_block(n2):
                        pool.wait_ge(high_ready, n2 + 1)
                        at_least(pool, low_ready, n2 - 2)
                        g.tensor_tensor(rest[u2][:, :, :], feats[u2][:, :, :], m.coded[u2][:, :, 0:FEATS], ALU.subtract).then_inc(high_off, 1)
                    if is_block(n1):
                        gather(range(SLOTS // 2, SLOTS))
                    if is_block(n2):
                        pool.wait_ge(mid_ready, n2 + 1)
                        g.tensor_tensor(rest[u2][:, :, :], rest[u2][:, :, :], m.coded[u2][:, :, 3 * FEATS:4 * FEATS], ALU.subtract).then_inc(mid_off, 1)
                    if is_block(na):
                        at_least(pool, runs_in[ua], 32 * qa)
                        at_least(pool, picked, 2 * (na - 2))
                        g.tensor_copy(facts[ua][:, :], m.facts[:, bass.ds(na, 1), :].rearrange("p a c -> p (a c)")).then_inc(facts_ready, 1)
                        pool.wait_ge(facts_ready, na + 1)
                        at_least(pool, sources_in[ua], SLOTS * 16 * qa)
                        at_least(pool, kept, na - 2)
                        at_least(pool, high_ready, na - 2)
                        at_least(pool, high_off, na - 2)
                        pool.sem_inc(pool_passed, 1)
                        pool.indirect_dma_start(ids[ua][:, :, :].rearrange("p s c -> p (s c)"), None, d.ids,
                                                bass.IndirectOffsetOnAxis(facts[ua][:, 0:1], 0)).then_inc(runs_in[ua], 16)
                        pool.indirect_dma_start(feats[ua][:, :, :].rearrange("p s f -> p (s f)"), None, d.efeat,
                                                bass.IndirectOffsetOnAxis(facts[ua][:, 0:1], 0)).then_inc(runs_in[ua], 16)
                steps(pool, step)

            @block.scalar
            def _(act):
                a = nc.scalar

                def step(q, u):
                    q1, u1, n1 = shifted_by(q, u, 1)
                    q2, u2, n2 = shifted_by(q, u, 2)
                    q3, u3, n3 = shifted_by(q, u, -3)
                    q4, u4, n4 = shifted_by(q, u, -4)
                    n = q * RING + u
                    if is_block(n3):
                        act.wait_ge(summed, n3 + 1)
                        at_least(act, sums_turned, n3 - 2)
                        a.activation(sums[u3][:, :], sums_ps[:, :], ACT.Copy).then_inc(sums_ready, 1)
                    if is_block(n):
                        act.wait_ge(sources_in[u], SLOTS * 16 * q + SLOTS * 16)
                        at_least(act, summed, n - 2)
                        for s in ACT_SLOTS:
                            act.wait_ge(weights_made, SLOTS * n + s + 1)
                            for i in range(FEATS):
                                last = a.activation(pair[u][:, s, :, i * FEATS:(i + 1) * FEATS],
                                                    act_ps[:, :].rearrange("p (c n) -> p c n", c=2)[:, :, i * FEATS:(i + 1) * FEATS],
                                                    ACT.Copy, scale=sources[u][:, s, i:i + 1])
                            last.then_inc(act_made, 1)
                    if is_block(n2):
                        act.wait_ge(picked, 2 * n2 + 2)
                        at_least(act, feats_turned, n2 - 2)
                        a.activation(m.coded[u2][:, :, 0:3 * FEATS].rearrange("p s (c f) -> p s c f", f=FEATS),
                                     feats[u2][:, :, :].unsqueeze(2).broadcast_to([128, SLOTS, 3, FEATS]), ACT.Copy).then_inc(high_ready, 1)
                    if is_block(n1):
                        act.wait_ge(feats_turned, n1 + 1)
                        at_least(act, weights_made, SLOTS * (n1 - 2))
                        a.activation(turned[u1][:, :, :], turn_ps, ACT.Copy).then_inc(feats_ready, 1)
                    if is_block(n3):
                        act.wait_ge(below_ready, n3 + 1)
                        a.activation(below[u3][:, :, :], below[u3][:, :, :], ACT.Exp).then_inc(below_raised, 1)
                        act.wait_ge(drop_ready, n3 + 1)
                        a.activation(drop[u3][:, :, :], drop[u3][:, :, :], ACT.Exp).then_inc(drop_raised, 1)
                    if is_block(n2):
                        act.wait_ge(high_off, n2 + 1)
                        a.activation(m.coded[u2][:, :, 3 * FEATS:5 * FEATS].rearrange("p s (c f) -> p s c f", f=FEATS),
                                     rest[u2][:, :, :].unsqueeze(2).broadcast_to([128, SLOTS, 2, FEATS]), ACT.Copy).then_inc(mid_ready, 1)
                    if is_block(n):
                        act.wait_ge(shifted, n + 1)
                        for s in range(SLOTS):
                            ex = pair[u][:, s, 0, :]
                            off = m.off[:, bass.ds(n, 1), s]
                            a.activation(ex, ex, ACT.Exp, bias=off).then_inc(raised, 1)
                    if is_block(n2):
                        act.wait_ge(mid_off, n2 + 1)
                        a.activation(m.coded[u2][:, :, 5 * FEATS:6 * FEATS], rest[u2][:, :, :], ACT.Copy).then_inc(low_ready, 1)
                    if is_block(n4):
                        act.wait_ge(joined_turned, n4 + 1)
                        at_least(act, out_stored[u4], 16 * q4)
                        a.activation(stored[u4][:, :, :], back_ps, ACT.Copy).then_inc(out_ready, 1)
                steps(act, step)

            @block.tensor
            def _(pe):
                t = nc.tensor

                def step(q, u):
                    q1, u1, n1 = shifted_by(q, u, 1)
                    q2, u2, n2 = shifted_by(q, u, -2)
                    q3, u3, n3 = shifted_by(q, u, -3)
                    q4, u4, n4 = shifted_by(q, u, -4)
                    n = q * RING + u
                    if is_block(n):
                        pe.wait_ge(feats_ready, n + 1)
                        for s in range(SLOTS):
                            if s in VEC_SLOTS:
                                j = VEC_SLOTS.index(s)
                                bank = vec_ps[j % 2]
                                at_least(pe, vec_made, n * len(VEC_SLOTS) + max(j - 1, 0))
                            else:
                                bank = act_ps
                                at_least(pe, act_made, n * len(ACT_SLOTS) + ACT_SLOTS.index(s))
                            t.matmul(bank[:, :], turned[u][:, s, :], m.coded_w[:, :], start=True, stop=True).then_inc(weights_made, 1)
                    if is_block(n3):
                        at_least(pe, below_ready, n3)
                        for h in range(2):
                            t.transpose(peak_t_ps[:, h, :], row_peak[u3][:, h * 128:(h + 1) * 128], m.ident[:, :])
                        pe.wait_ge(sums_ready, n3 + 1)
                        at_least(pe, sums_scaled, n3)
                        for k in range(4):
                            last = t.transpose(sums_t_ps[:, k, :], sums[u3][:, k * 128:(k + 1) * 128], m.ident[:, :])
                        last.then_inc(sums_turned, 1)
                    if is_block(n1):
                        pe.wait_ge(low_ready, n1 + 1)
                        at_least(pe, feats_ready, n1)
                        for s in range(SLOTS):
                            last = t.transpose(turn_ps[:, s, :], m.coded[u1][:, s, :], m.ident16[:, :])
                        last.then_inc(feats_turned, 1)
                    if is_block(n2):
                        pe.wait_ge(weighed, n2 + 1)
                        at_least(pe, sums_ready, n2)
                        for s in range(SLOTS):
                            last = t.matmul(sums_ps[:, :], m.ident[:, :], pair[u2][:, s, :, :].rearrange("p c n -> p (c n)"),
                                            start=(s == 0), stop=(s == SLOTS - 1))
                        last.then_inc(summed, 1)
                    if is_block(n4):
                        pe.wait_ge(joined, n4 + 1)
                        at_least(pe, out_ready, n4)
                        for k in range(4):
                            last = t.transpose(back_ps[:, k, :], m.carried[u4][:, k, :], m.ident[:, :])
                        last.then_inc(joined_turned, 1)
                steps(pe, step)

            @block.vector
            def _(dve):
                v = nc.vector

                def step(q, u):
                    q2, u2, n2 = shifted_by(q, u, 2)
                    q1, u1, n1 = shifted_by(q, u, -1)
                    q3, u3, n3 = shifted_by(q, u, -3)
                    n = q * RING + u
                    if is_block(n):
                        dve.wait_ge(sources_in[u], SLOTS * 16 * q + SLOTS * 16)
                        at_least(dve, summed, n - 2)
                        for j, s in enumerate(VEC_SLOTS):
                            dve.wait_ge(weights_made, SLOTS * n + s + 1)
                            v.tensor_tensor(pair[u][:, s, :, :].rearrange("p c (i o) -> p c i o", o=FEATS),
                                            vec_ps[j % 2][:, :].rearrange("p (c i o) -> p c i o", c=2, o=FEATS),
                                            sources[u][:, s, :].unsqueeze(1).unsqueeze(3).broadcast_to([128, 2, FEATS, FEATS]),
                                            ALU.mult).then_inc(vec_made, 1)
                    if is_block(n2):
                        dve.wait_ge(runs_in[u2], 32 * q2 + 32)
                        dve.wait_ge(facts_ready, n2 + 1)
                        dve.sem_inc(dve_passed, 1)
                        free = facts[u2][:, 2:1 + SLOTS].unsqueeze(2)
                        v.copy_predicated(ids[u2][:, 1:SLOTS, :], free.broadcast_to([128, SLOTS - 1, 2]),
                                          ids[u2][:, 0:1, :].broadcast_to([128, SLOTS - 1, 2])).then_inc(picked, 1)
                        v.copy_predicated(feats[u2][:, 1:SLOTS, :], free.broadcast_to([128, SLOTS - 1, FEATS]),
                                          feats[u2][:, 0:1, :].broadcast_to([128, SLOTS - 1, FEATS])).then_inc(picked, 1)
                        dve.wait_ge(picked, 2 * n2 + 1)
                        v.tensor_copy(m.edge_ids[:, bass.ds(n2, 1), :, :].rearrange("p a s c -> p (a s c)"),
                                      ids[u2][:, :, :].rearrange("p s c -> p (s c)")).then_inc(kept, 1)
                    if is_block(n3):
                        dve.wait_ge(sums_turned, n3 + 1)
                        dve.wait_ge(restart_in[u3], 16 * q3 + 16)
                        at_least(dve, drop_ready, n3 - 2)
                        before = m.peak[(u3 - 1) % RING]
                        at_least(dve, peak_run, 3 * n3)
                        at_least(dve, below_ready, n3 - 2)
                        v.tensor_copy(m.peak[u3][:, :, 0:1], before[:, :, 128:129]).then_inc(peak_run, 1)
                        for h in range(2):
                            v.tensor_tensor_scan(m.peak[u3][:, h, 1:129], restart[u3][:, :], peak_t_ps[:, h, :],
                                                 before[:, h, 128:129], ALU.add, ALU.max).then_inc(peak_run, 1)
                        at_least(dve, sums_scaled, n3 - 2)
                    if is_block(n):
                        dve.wait_ge(vec_made, len(VEC_SLOTS) * (n + 1))
                        dve.wait_ge(act_made, len(ACT_SLOTS) * (n + 1))
                        at_least(dve, sums_turned, n - 2)
                        v.tensor_reduce(row_peak[u][:, :], pair[u][:, :, 0, :].rearrange("p s c -> p c s"), X, ALU.max).then_inc(row_peaked, 1)
                    if is_block(n3):
                        dve.wait_ge(peak_run, 3 * n3 + 3)
                        v.tensor_tensor(below[u3][:, :, :], peak_t_ps, m.peak[u3][:, :, 1:129], ALU.subtract).then_inc(below_ready, 1)
                    if is_block(n):
                        dve.wait_ge(row_peaked, n + 1)
                        v.tensor_tensor(pair[u][:, :, 0, :], pair[u][:, :, 0, :],
                                        row_peak[u][:, :].unsqueeze(1).broadcast_to([128, SLOTS, CHANNELS]), ALU.subtract).then_inc(shifted, 1)
                    if is_block(n1):
                        dve.wait_ge(raised, SLOTS * n1 + SLOTS)
                        v.tensor_tensor(pair[u1][:, :, 1, :], pair[u1][:, :, 1, :], pair[u1][:, :, 0, :], ALU.mult).then_inc(weighed, 1)
                    if is_block(n3):
                        dve.wait_ge(below_raised, n3 + 1)
                        v.tensor_tensor(scaled[u3][:, :, :].rearrange("p (c h) r -> p c h r", h=2),
                                        sums_t_ps.rearrange("p (c h) r -> p c h r", h=2),
                                        below[u3][:, :, :].unsqueeze(1).broadcast_to([128, 2, 2, 128]), ALU.mult).then_inc(sums_scaled, 1)
                        dve.wait_ge(sums_scaled, n3 + 1)
                        dve.wait_ge(drop_raised, n3 + 1)
                        at_least(dve, joined_turned, n3 - 2)
                        before = m.carried[(u3 - 1) % RING]
                        for k in range(4):
                            last = v.tensor_tensor_scan(m.carried[u3][:, k, :], drop[u3][:, k % 2, :], scaled[u3][:, k, :],
                                                        before[:, k, 127:128], ALU.mult, ALU.add)
                        last.then_inc(joined, 1)
                steps(dve, step)


def norm_vector(v, eng, chain, t, spread_ready, root_ready):
    wide = [NP, NB, FEATS]
    chain(v.tensor_reduce(t.mean[:, :], t.x[:, :, :], X, ALU.add))
    chain(v.tensor_scalar(t.mean[:, :], t.mean[:, :], 1.0 / FEATS, None, ALU.mult))
    chain(v.tensor_tensor(t.x[:, :, :], t.x[:, :, :], t.mean[:, :].unsqueeze(2).broadcast_to(wide), ALU.subtract))
    chain(v.tensor_tensor(t.square[:, :, :], t.x[:, :, :], t.x[:, :, :], ALU.mult))
    chain(v.tensor_reduce(t.mean[:, :], t.square[:, :, :], X, ALU.add))
    v.tensor_scalar(t.mean[:, :], t.mean[:, :], 1.0 / FEATS, EPS, ALU.mult, ALU.add).then_inc(spread_ready, 1)
    eng.wait_ge(root_ready, 1)
    chain(v.reciprocal(t.root[:, :], t.root[:, :]))
    return v.tensor_tensor(t.out[:, :, :], t.x[:, :, :], t.root[:, :].unsqueeze(2).broadcast_to(wide), ALU.mult)


def last_sums(nc, m, sem):
    def sb(name, shape, dt=F32):
        return m.ctx.enter_context(nc.sbuf_tensor(name, shape, dt))

    l = Tensors()
    l.group = 5
    l.chunks = NB // l.group
    l.by_pool = 2
    l.rows = sb("last_rows", [NP, NB, 2, CHANNELS])
    l.inverse = sb("inverse", [NP, NB, CHANNELS])
    l.rows_in = [sem(f"node_sums_in{i}") for i in range(l.chunks)]
    l.logs, l.inverted, l.multiplied = sem("logs"), sem("inverted"), sem("multiplied")
    return l


def fetch_last_sums(nc, m, l, pool):
    for b in range(NB):
        pool.indirect_dma_start(l.rows[:, b, :, :].rearrange("p c n -> p (c n)"), None, m.row_sums,
                                bass.IndirectOffsetOnAxis(m.node_last[:, b:b + 1], 0)).then_inc(l.rows_in[b // l.group], 16)


def invert_last_sums(nc, l, act):
    for c in range(l.chunks):
        group = slice(c * l.group, (c + 1) * l.group)
        act.wait_ge(l.rows_in[c], 16 * l.group)
        nc.scalar.activation(l.inverse[:, group, :], l.rows[:, group, 0, :], ACT.Ln).then_inc(l.logs, 1)
    for c in range(l.chunks):
        group = slice(c * l.group, (c + 1) * l.group)
        act.wait_ge(l.logs, c + 1)
        nc.scalar.activation(l.inverse[:, group, :], l.inverse[:, group, :], ACT.Exp, scale=-1.0).then_inc(l.inverted, 1)


def multiply_last_sums(nc, l, pool):
    for c in range(l.chunks):
        group = slice(c * l.group, (c + 1) * l.group)
        pool.wait_ge(l.inverted, c + 1)
        last = nc.gpsimd.tensor_tensor(l.rows[:, group, 1, :], l.rows[:, group, 1, :], l.inverse[:, group, :], ALU.mult)
        if c < l.by_pool:
            last = nc.gpsimd.tensor_tensor(l.rows[:, group, 0, :], l.rows[:, group, 0, :], l.inverse[:, group, :], ALU.mult)
        last.then_inc(l.multiplied, 1)


def finish_attention(nc, d, m, sem, l):
    ctx = ExitStack()
    with ctx:
        def sb(name, shape, dt=F32):
            return ctx.enter_context(nc.sbuf_tensor(name, shape, dt))

        node_sum = sb("node_sum", [NP, NB, FEATS])
        t = Tensors()
        t.x, t.out = m.node_x, m.node_x
        t.mean, t.root, t.square = sb("mean0", [NP, NB]), sb("root0", [NP, NB]), sb("square0", [NP, NB, FEATS])
        spread_ready, root_ready, chain_sem = sem("spread_ready0"), sem("root_ready0"), sem("norm0_chain")
        with nc.Block() as block:
            @block.scalar
            def _(act):
                act.wait_ge(spread_ready, 1)
                nc.scalar.activation(t.root[:, :], t.mean[:, :], ACT.Sqrt).then_inc(root_ready, 1)

            @block.vector
            def _(dve):
                chain = Chain(dve, chain_sem)
                v = nc.vector
                for c in range(l.chunks):
                    group = slice(c * l.group, (c + 1) * l.group)
                    s_r, q = l.rows[:, group, 0, :], l.rows[:, group, 1, :]
                    dve.wait_ge(l.multiplied, c + 1)
                    if c >= l.by_pool:
                        chain(v.tensor_tensor(s_r, s_r, l.inverse[:, group, :], ALU.mult))
                    chain(v.scalar_tensor_tensor(q, s_r, -2.0, q, ALU.add, ALU.mult))
                    chain(v.tensor_reduce(node_sum[:, group, :], q.rearrange("p b (i o) -> p b o i", o=FEATS), X, ALU.add))
                chain(v.tensor_tensor(node_sum[:, :, :], node_sum[:, :, :], m.node_has[:, :].unsqueeze(2).broadcast_to([NP, NB, FEATS]), ALU.mult))
                chain(v.tensor_tensor(m.node_x[:, :, :], m.node_x[:, :, :], node_sum[:, :, :], ALU.subtract))
                chain(norm_vector(v, dve, chain, t, spread_ready, root_ready))


def segment_sums(nc, m, sem, values, width, table, tag, totals=None):
    ctx = ExitStack()
    with ctx:
        def sb(name, shape, dt=F32):
            return ctx.enter_context(nc.sbuf_tensor(f"{tag}_{name}", shape, dt))

        run = sb("run", [BLOCKS, 128, width])
        through = sb("through", [BLOCKS, 128])
        both = sb("both", [BLOCKS, 2, width])
        last_t = sb("last_t", [width, 2, BLOCKS])
        carry_t = sb("carry_t", [width, BLOCKS + 1])
        carry = sb("carry", [BLOCKS, width])
        chain_sem, turned, ends_ready, ends_turned = sem(f"{tag}_chain"), sem(f"{tag}_turned"), sem(f"{tag}_ends_ready"), sem(f"{tag}_ends_turned")
        carry_ready, carry_turned, run_ready, stored = sem(f"{tag}_carry_ready"), sem(f"{tag}_carry_turned"), sem(f"{tag}_run_ready"), sem(f"{tag}_stored")
        turned_ps = [m.psum[f // 4][0:BLOCKS, (f % 4) * 128:(f % 4 + 1) * 128] for f in range(width)]
        ends_ps = [m.psum[5 + i][0:width, 0:BLOCKS] for i in range(2)]
        carry_ps = m.psum[7][0:BLOCKS, 0:width]
        if totals is not None:
            after = sb("after", [BLOCKS, width, 128])
            back = sb("back", [BLOCKS, 128])
            heads = sb("heads", [BLOCKS, width])
            heads_t = sb("heads_t", [width, BLOCKS])
            next_t = sb("next_t", [width, BLOCKS + 1])
            heads_ready, heads_turned, next_ready, next_turned = (sem(f"{tag}_{x}") for x in ("heads_ready", "heads_turned", "next_ready", "next_turned"))
            whole_ready, whole_turned = sem(f"{tag}_whole_ready"), sem(f"{tag}_whole_turned")
            whole_ps = [m.psum[f // 4][:, (f % 4) * BLOCKS:(f % 4 + 1) * BLOCKS] for f in range(width)]

        with nc.Block() as block:
            @block.tensor
            def _(pe):
                t = nc.tensor
                for f in range(width):
                    last = t.transpose(turned_ps[f], values[:, f, :], m.ident[:, :])
                last.then_inc(turned, 1)
                pe.wait_ge(ends_ready, 1)
                for i in range(2):
                    last = t.transpose(ends_ps[i], both[:, i, :], m.ident[0:BLOCKS, 0:BLOCKS])
                last.then_inc(ends_turned, 1)
                pe.wait_ge(carry_ready, 1)
                t.transpose(carry_ps, carry_t[:, 0:BLOCKS], m.ident[0:width, 0:width]).then_inc(carry_turned, 1)
                if totals is not None:
                    pe.wait_ge(heads_ready, 1)
                    t.transpose(ends_ps[0], heads[:, :], m.ident[0:BLOCKS, 0:BLOCKS]).then_inc(heads_turned, 1)
                    pe.wait_ge(next_ready, 1)
                    t.transpose(carry_ps, next_t[:, 1:BLOCKS + 1], m.ident[0:width, 0:width]).then_inc(next_turned, 1)
                    pe.wait_ge(whole_ready, 1)
                    for f in range(width):
                        last = t.transpose(whole_ps[f], after[:, f, :], m.ident[0:BLOCKS, 0:BLOCKS])
                    last.then_inc(whole_turned, 1)

            @block.vector
            def _(dve):
                chain = Chain(dve, chain_sem)
                v = nc.vector
                keep = m.keep[:, 0:128]
                chain(v.tensor_tensor_scan(through[:, :], keep, keep, 1.0, ALU.mult, ALU.min))
                chain(v.tensor_copy(both[:, 1, :], through[:, 127:128].broadcast_to([BLOCKS, width])))
                dve.wait_ge(turned, 1)
                for f in range(width):
                    chain(v.tensor_tensor_scan(run[:, :, f], keep, turned_ps[f], 0.0, ALU.mult, ALU.add))
                v.tensor_copy(both[:, 0, :], run[:, 127, :]).then_inc(ends_ready, 1)
                dve.wait_ge(ends_turned, 1)
                for i in range(2):
                    chain(v.tensor_copy(last_t[:, i, :], ends_ps[i]))
                chain(v.memset(carry_t[:, 0:1], 0.0))
                v.tensor_tensor_scan(carry_t[:, 1:BLOCKS + 1], last_t[:, 1, :], last_t[:, 0, :], 0.0, ALU.mult, ALU.add).then_inc(carry_ready, 1)
                dve.wait_ge(carry_turned, 1)
                chain(v.tensor_copy(carry[:, :], carry_ps))
                for f in range(width):
                    last = v.scalar_tensor_tensor(run[:, :, f], through[:, :], carry[:, f:f + 1], run[:, :, f], ALU.mult, ALU.add)
                last.then_inc(run_ready, 1)
                if totals is None:
                    return
                dve.wait_ge(run_ready, 1)
                keep_next = m.keep[:, 1:129][:, ::-1]
                for f in range(width):
                    chain(v.tensor_tensor_scan(after[:, f, ::-1], keep_next, run[:, ::-1, f], 0.0, ALU.mult, ALU.max))
                chain(v.tensor_tensor_scan(back[:, ::-1], keep_next, keep_next, 1.0, ALU.mult, ALU.min))
                v.tensor_scalar(heads[:, :], after[:, :, 0], m.keep[:, 0:1], None, ALU.mult).then_inc(heads_ready, 1)
                dve.wait_ge(heads_turned, 1)
                chain(v.tensor_copy(heads_t[:, :], ends_ps[0]))
                chain(v.memset(next_t[:, BLOCKS:BLOCKS + 1], 0.0))
                v.tensor_tensor_scan(next_t[:, 0:BLOCKS][:, ::-1], last_t[:, 1, ::-1], heads_t[:, ::-1], 0.0, ALU.mult, ALU.max).then_inc(next_ready, 1)
                dve.wait_ge(next_turned, 1)
                chain(v.tensor_copy(carry[:, :], carry_ps))
                for f in range(width):
                    last = v.scalar_tensor_tensor(after[:, f, :], back[:, :], carry[:, f:f + 1], after[:, f, :], ALU.mult, ALU.max)
                last.then_inc(whole_ready, 1)
                dve.wait_ge(whole_turned, 1)
                for f in range(width):
                    last = v.tensor_copy(totals[:, f, :], whole_ps[f])
                chain(last)

            if totals is None:
                @block.sync
                def _(sp):
                    sp.wait_ge(run_ready, 1)
                    sp.dma_start(table.rearrange("(p r) f -> p r f", r=128), run[:, :, :]).then_inc(stored, 16)
                    sp.wait_ge(stored, 16)


def relation_norms(nc, d, m, sem, l):
    ctx = ExitStack()
    with ctx:
        def sb(name, shape, dt=F32):
            return ctx.enter_context(nc.sbuf_tensor(name, shape, dt))

        counts = sb("counts", [128, RELATIONS, BLOCKS])
        types = sb("types", [128, BLOCKS, SLOTS])
        match = sb("match", [128, BLOCKS, SLOTS])
        source = sb("source", [128, BLOCKS, SLOTS])
        within = sb("within", [128, BLOCKS * SLOTS])
        within_t = sb("within_t", [BLOCKS, SLOTS, 128], F16)
        line_i = sb("line_i", [128, LINES], I32)
        page_i = sb("page_i", [128, PAGES], I32)
        count_chain, numbers_ready, counted = sem("match_chain"), sem("numbers_ready"), sem("counted")
        within_ready, within_turned, within_back, within_out = sem("within_ready"), sem("within_turned"), sem("within_back"), sem("within_out")
        whole = [128, BLOCKS, SLOTS]
        turned_ps = [m.psum[c][0:BLOCKS, 0:128] for c in range(SLOTS)]
        with nc.Block() as block:
            @block.gpsimd
            def _(pool):
                nc.gpsimd.iota(line_i[:, :], pattern=[[128, LINES]], base=0, channel_multiplier=1).then_inc(numbers_ready, 1)
                nc.gpsimd.iota(page_i[:, :], pattern=[[1, PAGES]], base=0, channel_multiplier=0).then_inc(numbers_ready, 1)
                fetch_last_sums(nc, m, l, pool)

            @block.tensor
            def _(pe):
                pe.wait_ge(within_ready, 1)
                for c in range(SLOTS):
                    nc.tensor.transpose(turned_ps[c], within[:, c * BLOCKS:(c + 1) * BLOCKS], m.ident[:, :]).then_inc(within_turned, 1)

            @block.scalar
            def _(act):
                for c in range(SLOTS):
                    act.wait_ge(within_turned, c + 1)
                    nc.scalar.activation(within_t[:, c, :], turned_ps[c], ACT.Copy).then_inc(within_back, 1)

            @block.sync
            def _(sp):
                sp.wait_ge(within_back, SLOTS)
                sp.dma_start(m.within_table.rearrange("(c p) r -> p c r", p=BLOCKS), within_t[:, :, :]).then_inc(within_out, 16)
                sp.wait_ge(within_out, 16)

            @block.vector
            def _(dve):
                chain = Chain(dve, count_chain)
                v = nc.vector
                chain(v.tensor_copy(source[:, :, :], m.edge_ids[:, :, :, 0]))
                chain(v.memset(m.page[:, :, :], 0.0))
                for h in range(1, PAGES):
                    chain(v.scalar_tensor_tensor(m.page[:, :, :], source[:, :, :], float(h * WITHIN), m.page[:, :, :], ALU.is_ge, ALU.add))
                v.scalar_tensor_tensor(within[:, :].rearrange("p (b s) -> p b s", s=SLOTS), m.page[:, :, :], -float(WITHIN), source[:, :, :],
                                       ALU.mult, ALU.add).then_inc(within_ready, 1)
                dve.wait_ge(numbers_ready, 2)
                chain(v.tensor_copy(m.line_no[:, :], line_i[:, :]))
                chain(v.tensor_scalar(m.minus_line[:, :], m.line_no[:, :], -1.0, None, ALU.mult))
                chain(v.tensor_copy(m.page_no[:, :], page_i[:, :]))
                chain(v.tensor_copy(types[:, :, :], m.edge_ids[:, :, :, 1]))
                chain(v.scalar_tensor_tensor(m.message_at[:, :, :], source[:, :, :], float(RELATIONS), types[:, :, :], ALU.mult, ALU.add))
                chain(v.scalar_tensor_tensor(types[:, :, :], types[:, :, :], 1.0, m.used[:, :, :], ALU.add, ALU.mult))
                chain(v.tensor_scalar(types[:, :, :], types[:, :, :], -1.0, None, ALU.add))
                for r in range(RELATIONS):
                    chain(v.tensor_scalar(match[:, :, :], types[:, :, :], float(r), None, ALU.is_equal))
                    chain(v.tensor_reduce(counts[:, r, :], match[:, :, :], X, ALU.add))
        segment_sums(nc, m, sem, counts, RELATIONS, None, "count", totals=counts)
        norm_chain = sem("norm_chain")
        with nc.Block() as block:
            @block.scalar
            def _(act):
                invert_last_sums(nc, l, act)

            @block.gpsimd
            def _(pool):
                multiply_last_sums(nc, l, pool)

            @block.vector
            def _(dve):
                chain = Chain(dve, norm_chain)
                v = nc.vector
                chain(v.tensor_scalar(counts[:, :, :], counts[:, :, :], 1.0, None, ALU.max))
                chain(v.reciprocal(counts[:, :, :], counts[:, :, :]))
                for r in range(RELATIONS):
                    chain(v.scalar_tensor_tensor(m.typed_norm[:, :, :, r], types[:, :, :], float(r), counts[:, r, :].unsqueeze(2).broadcast_to(whole), ALU.is_equal, ALU.mult))
                chain(v.tensor_reduce(m.norm[:, :, :], m.typed_norm[:, :, :, :], X, ALU.add))


def project(nc, d, m, sem, k):
    ctx = ExitStack()
    outs = RELATIONS * FEATS + FEATS
    x = m.node_x if k == 0 else m.hidden
    with ctx:
        def sb(name, shape, dt=F32):
            return ctx.enter_context(nc.sbuf_tensor(f"{name}{k}", shape, dt))

        x_t = sb("x_t", [FEATS + 1, NB, NP])
        paged = sb("paged", [128, PAGES, LINES, FEATS])
        rest = sb("paged_rest", [128, PAGES, LINES, FEATS])
        paged_clear, x_out, paged_in, split_chain = sem(f"paged_clear{k}"), sem(f"x_out{k}"), sem(f"paged_in{k}"), sem(f"split_chain{k}")
        loads = []
        for page in range(PAGES):
            left = min(WITHIN, NODES - page * WITHIN)
            loads.append((page, 0, left // 128, 128))
            if left % 128:
                loads.append((page, left // 128, 1, left % 128))
        weights = sb("layer_w", [FEATS + 1, outs])
        made = sb("made", [NP, NB, RELATIONS * FEATS])
        w_in, w_clear, ones_ready = sem(f"w_in{k}"), sem(f"w_clear{k}"), sem(f"ones_ready{k}")
        x_turned, x_ready, products, taken, table_out = sem(f"x_turned{k}"), sem(f"x_ready{k}"), sem(f"products{k}"), sem(f"taken{k}"), sem(f"table_out{k}")
        weights_in, root_in, bias_in = d.layers[k]
        GROUP = 3
        groups = [range(a, min(a + GROUP, NB)) for a in range(0, NB, GROUP)]
        with nc.Block() as block:
            @block.sync
            def _(sp):
                sp.dma_start(m.node_table[k].rearrange("(p b) f -> p b f", b=NB), x[:, :, :]).then_inc(x_out, 16)
                sp.dma_start(m.stacked_w[:, :], weights_in.rearrange("r i o -> (r i) o")).then_inc(w_in, 16)
                sp.wait_ge(w_clear, 1)
                sp.dma_start(weights[0:FEATS, 0:RELATIONS * FEATS].rearrange("i (r o) -> i r o", r=RELATIONS), weights_in.rearrange("r i o -> i r o")).then_inc(w_in, 16)
                sp.dma_start(weights[0:FEATS, RELATIONS * FEATS:], root_in).then_inc(w_in, 16)
                sp.dma_start(weights[FEATS:FEATS + 1, RELATIONS * FEATS:], bias_in.rearrange("(a n) -> a n", a=1)).then_inc(w_in, 16)
                sp.wait_ge(x_out, 16)
                sp.wait_ge(paged_clear, 1)
                for page, line, lines, rows in loads:
                    first = page * WITHIN + line * 128
                    sp.dma_start(paged[0:rows, page, line:line + lines, :],
                                 m.node_table[k][first:first + lines * rows, :].rearrange("(l p) f -> p l f", p=rows)).then_inc(paged_in, 16)
                sp.wait_ge(taken, len(groups))
                sp.dma_start(m.projected[k].rearrange("(p b r) o -> p b r o", b=NB, r=RELATIONS).rearrange("p b r o -> p (b r o)"),
                             made[:, :, :].rearrange("p b n -> p (b n)")).then_inc(table_out, 16)
                sp.wait_ge(table_out, 16)

            @block.gpsimd
            def _(pool):
                nc.gpsimd.memset(paged[:, :, :, :], 0.0).then_inc(paged_clear, 1)
                nc.gpsimd.memset(weights[:, :], 0.0).then_inc(w_clear, 1)
                nc.gpsimd.memset(x_t[:, :, :], 1.0).then_inc(ones_ready, 1)

            @block.tensor
            def _(pe):
                t = nc.tensor
                for b in range(NB):
                    if b >= 8:
                        pe.wait_ge(x_ready, b - 7)
                    t.transpose(m.psum[b % 8][0:FEATS, 0:NP], x[:, b, :], m.ident[0:NP, 0:NP]).then_inc(x_turned, 1)
                pe.wait_ge(w_in, 64)
                for n, group in enumerate(groups):
                    pe.wait_ge(x_ready, NB)
                    if n >= 8:
                        pe.wait_ge(taken, n - 7)
                    for i, b in enumerate(group):
                        last = t.matmul(m.psum[n % 8][0:NP, i * outs:(i + 1) * outs], x_t[:, b, :], weights[:, :], start=True, stop=True)
                    last.then_inc(products, 1)

            @block.vector
            def _(dve):
                v = nc.vector
                dve.wait_ge(ones_ready, 1)
                for b in range(NB):
                    dve.wait_ge(x_turned, b + 1)
                    v.tensor_copy(x_t[0:FEATS, b, :], m.psum[b % 8][0:FEATS, 0:NP]).then_inc(x_ready, 1)
                for n, group in enumerate(groups):
                    dve.wait_ge(products, n + 1)
                    bank = m.psum[n % 8][0:NP, 0:len(group) * outs].rearrange("p (b n) -> p b n", n=outs)
                    v.tensor_copy(m.rooted[:, group[0]:group[-1] + 1, :], bank[:, :, RELATIONS * FEATS:])
                    v.tensor_copy(made[:, group[0]:group[-1] + 1, :], bank[:, :, 0:RELATIONS * FEATS]).then_inc(taken, 1)
                chain = Chain(dve, split_chain)
                dve.wait_ge(paged_in, 16 * len(loads))
                parts = [m.x_parts[:, i, :, :].rearrange("p l (g f) -> p g l f", f=FEATS) for i in range(3)]
                chain(v.tensor_copy(parts[0], paged[:, :, :, :]))
                chain(v.tensor_tensor(rest[:, :, :, :], paged[:, :, :, :], parts[0], ALU.subtract))
                chain(v.tensor_copy(parts[1], rest[:, :, :, :]))
                chain(v.tensor_tensor(rest[:, :, :, :], rest[:, :, :, :], parts[1], ALU.subtract))
                chain(v.tensor_copy(parts[2], rest[:, :, :, :]))


def gather_messages(nc, m, sem, sems, k):
    ctx = ExitStack()
    PAIR = 2
    WEIGHED = MATRIX_TURNS * (LAPS - 1) + sum(at < LEFT for at in MATRIX_AT)
    FETCHED = TABLE_TURNS * (LAPS - 1) + sum(at < LEFT for at in TABLE_AT)
    HALF = SLOTS // 2
    with ctx:
        def ring(name, shape, dt=F32, n=PAIR):
            return [ctx.enter_context(nc.sbuf_tensor(f"{name}{k}_{u}", shape, dt)) for u in range(n)]

        def sem_k(name):
            return sem(f"{name}{k}")

        at = ring("at", [128, SLOTS], I32, TABLE_TURNS)
        got = ring("got", [128, SLOTS, FEATS], F32, TABLE_TURNS)
        within = ring("within_at", [128, SLOTS * 128], F16)
        hot = ring("hot", [128, LINES, SLOTS * 128], BF16)
        distance = ring("distance", [128, SLOTS * 128], BF16, len(ACT_LINES))
        on_page = ring("on_page", [128, SLOTS, PAGES])
        paged = ring("picked_pages", [128, SLOTS, PAGES, FEATS])
        picked = ring("picked_x", [128, SLOTS, FEATS])
        typed = ring("typed", [128, RELATIONS, FEATS, SLOTS])
        rows = ring("typed_rows", [128, RELATIONS * FEATS])
        rows_t = ring("typed_rows_t", [RELATIONS * FEATS, 128])
        picked_ps = [[m.psum[2 * u + i][:, 0:HALF * PAGES * FEATS] for i in range(2)] for u in range(PAIR)]
        turned_ps, made_ps = m.psum[4][:, 0:128], m.psum[5][:, 0:FEATS]

        at_ready, weighted, reduced, passed = sem_k("at_ready"), sem_k("weighted"), sem_k("reduced"), sem_k("pool_passed")
        got_in = [sem_k(f"got_in{i}_") for i in range(TABLE_TURNS)]
        within_in = [sem_k(f"within_in{u}_") for u in range(PAIR)]
        distance_ready, act_hot_ready = sem_k("distance_ready"), sem_k("act_hot_ready")
        hot_ready, picks_made, pages_known, pages_kept = sem_k("hot_ready"), sem_k("picks_made"), sem_k("pages_known"), sem_k("pages_kept")
        picks_ready, typed_ready, rows_ready, rows_turned = sem_k("picks_ready"), sem_k("typed_ready"), sem_k("rows_ready"), sem_k("rows_turned")
        rows_back, made, kept = sem_k("rows_back"), sem_k("made"), sem_k("kept")

        def counted(lap, i):
            lap, i = lap + i // MATRIX_TURNS, i % MATRIX_TURNS
            return lap * MATRIX_TURNS + i, lap * TURNS + MATRIX_AT[i], i % PAIR, lap * (MATRIX_TURNS // PAIR) + i // PAIR

        def is_one(w, of=WEIGHED):
            return not isinstance(w, int) or 0 <= w < of

        def laps(eng, lap):
            lap(0)
            with eng.Fori(1, LAPS - 1) as q:
                lap(q)
            lap(LAPS - 1)

        with nc.Block() as block:
            @block.gpsimd
            def _(pool):
                def next_of(q, i):
                    return q + (i + 1) // TABLE_TURNS, (i + 1) % TABLE_TURNS

                def place(q, i):
                    if is_one(TABLE_TURNS * q + i, FETCHED):
                        at_least(pool, got_in[i], 16 * SLOTS * q)
                        nc.gpsimd.tensor_copy(at[i][:, :], m.message_at[:, bass.ds(TURNS * q + TABLE_AT[i], 1), :].rearrange("p a s -> p (a s)")).then_inc(at_ready, 1)

                def lap(q):
                    for i in range(TABLE_TURNS):
                        place(*next_of(q, i))
                        if not is_one(TABLE_TURNS * q + i, FETCHED):
                            continue
                        pool.wait_ge(at_ready, TABLE_TURNS * q + i + 1)
                        at_least(pool, reduced, TABLE_TURNS * (q - 1) + i + 1)
                        pool.sem_inc(passed, 1)
                        for s in range(SLOTS):
                            pool.indirect_dma_start(got[i][:, s, :], None, m.projected[k], bass.IndirectOffsetOnAxis(at[i][:, s:s + 1], 0)).then_inc(got_in[i], 16)
                place(0, 0)
                laps(pool, lap)

            @block.sync
            def _(sp):
                def lap(q):
                    for i in range(MATRIX_TURNS):
                        w, n, u, uses = counted(q, i)
                        if not is_one(w):
                            continue
                        at_least(sp, hot_ready, w - PAIR + 1)
                        at_least(sp, act_hot_ready, w - PAIR + 1)
                        sp.dma_start(within[u][:, :], m.within_table[bass.ds(SLOTS * n, SLOTS), :].rearrange("s r -> (s r)").partition_broadcast(128)).then_inc(within_in[u], 16)
                laps(sp, lap)

            @block.tensor
            def _(pe):
                t = nc.tensor

                def step(q, i):
                    w, n, u, uses = counted(q, i)
                    w1, n1, u1, uses1 = counted(q, i - 1)
                    w2, n2, u2, uses2 = counted(q, i - 2)
                    if is_one(w):
                        pe.wait_ge(hot_ready, w + 1)
                        pe.wait_ge(act_hot_ready, w + 1)
                        at_least(pe, pages_kept, 2 * (w - PAIR + 1))
                        for s in range(SLOTS):
                            out = picked_ps[u][s // HALF][:, (s % HALF) * PAGES * FEATS:(s % HALF + 1) * PAGES * FEATS]
                            for line in range(LINES):
                                for part in range(3):
                                    last = t.matmul(out, hot[u][:, line, s * 128:(s + 1) * 128], m.x_parts[:, part, line, :],
                                                    start=(line == 0 and part == 0), stop=(line == LINES - 1 and part == 2))
                            if s % HALF == HALF - 1:
                                last.then_inc(picks_made, 1)
                    if is_one(w1):
                        pe.wait_ge(rows_ready, w1 + 1)
                        at_least(pe, rows_back, w1)
                        t.transpose(turned_ps, rows[u1][:, :], m.ident[:, :]).then_inc(rows_turned, 1)
                    if is_one(w2):
                        pe.wait_ge(rows_back, w2 + 1)
                        at_least(pe, kept, w2)
                        t.matmul(made_ps, rows_t[u2][:, :], m.stacked_w[:, :], start=True, stop=True).then_inc(made, 1)

                laps(pe, lambda q: [step(q, i) for i in range(MATRIX_TURNS)])
                for i in range(2):
                    step(LAPS, i)

            @block.scalar
            def _(act):
                def make_hot(q, i):
                    w, n, u, uses = counted(q, i)
                    if not is_one(w):
                        return
                    act.wait_ge(within_in[u], 16 * (uses + 1))
                    at_least(act, act_hot_ready, w)
                    for j, line in enumerate(ACT_LINES):
                        nc.scalar.activation(distance[j][:, :], within[u][:, :], ACT.Abs, bias=m.minus_line[:, line:line + 1]).then_inc(distance_ready, 1)
                    at_least(act, picks_made, 2 * (w - PAIR + 1))
                    for j, line in enumerate(ACT_LINES):
                        act.wait_ge(distance_ready, len(ACT_LINES) * w + j + 1)
                        last = nc.scalar.activation(hot[u][:, line, :], distance[j][:, :], ACT.Relu, bias=1.0, scale=-1.0)
                    last.then_inc(act_hot_ready, 1)

                def step(q, i):
                    make_hot(q, i + PAIR)
                    w1, n1, u1, uses1 = counted(q, i - 1)
                    w2, n2, u2, uses2 = counted(q, i - 2)
                    if is_one(w1):
                        act.wait_ge(rows_turned, w1 + 1)
                        at_least(act, made, w1 - PAIR + 1)
                        nc.scalar.activation(rows_t[u1][:, :], turned_ps, ACT.Copy).then_inc(rows_back, 1)
                    if is_one(w2):
                        act.wait_ge(made, w2 + 1)
                        nc.scalar.activation(m.messages[:, :, bass.ds(n2, 1)].rearrange("p f a -> p (f a)"), made_ps, ACT.Copy).then_inc(kept, 1)

                for i in range(PAIR):
                    make_hot(0, i)
                laps(act, lambda q: [step(q, i) for i in range(MATRIX_TURNS)])
                for i in range(2):
                    step(LAPS, i)

            @block.vector
            def _(dve):
                v = nc.vector

                def make_hot(q, i, lines):
                    w, n, u, uses = counted(q, i)
                    if not is_one(w):
                        return
                    if 0 in lines:
                        dve.wait_ge(within_in[u], 16 * (uses + 1))
                        at_least(dve, picks_made, 2 * (w - PAIR + 1))
                    for line in lines:
                        last = v.tensor_scalar(hot[u][:, line, :], within[u][:, :], m.line_no[:, line:line + 1], None, ALU.is_equal)
                    if VEC_LINES[-1] in lines:
                        last.then_inc(hot_ready, 1)

                def weigh_got(q, i):
                    n, w = TURNS * q + TABLE_AT[i], TABLE_TURNS * q + i
                    if is_one(w, FETCHED):
                        dve.wait_ge(got_in[i], 16 * SLOTS * (q + 1))
                        norm = m.norm[:, bass.ds(n, 1), :].rearrange("p a s -> p (a s)").unsqueeze(2).broadcast_to([128, SLOTS, FEATS])
                        v.tensor_tensor(got[i][:, :, :], got[i][:, :, :], norm, ALU.mult).then_inc(weighted, 1)

                def sum_got(q, i):
                    n, w = TURNS * q + TABLE_AT[i], TABLE_TURNS * q + i
                    if is_one(w, FETCHED):
                        dve.wait_ge(weighted, w + 1)
                        v.tensor_reduce(m.messages[:, :, bass.ds(n, 1)].rearrange("p f a -> p (f a)"), got[i][:, :, :].rearrange("p s f -> p f s"), X, ALU.add).then_inc(reduced, 1)

                def from_products(q, i, between):
                    w, n, u, uses = counted(q, i)
                    page = m.page[:, bass.ds(n, 1), :].rearrange("p a s -> p (a s)").unsqueeze(2).broadcast_to([128, SLOTS, PAGES])
                    v.tensor_tensor(on_page[u][:, :, :], page, m.page_no[:, :].unsqueeze(1).broadcast_to([128, SLOTS, PAGES]), ALU.is_equal).then_inc(pages_known, 1)
                    between(0)
                    dve.wait_ge(pages_known, w + 1)
                    for h in range(2):
                        dve.wait_ge(picks_made, 2 * w + h + 1)
                        part = slice(h * HALF, (h + 1) * HALF)
                        v.tensor_tensor(paged[u][:, part, :, :], picked_ps[u][h].rearrange("p (s g f) -> p s g f", s=HALF, f=FEATS),
                                        on_page[u][:, part, :].unsqueeze(3).broadcast_to([128, HALF, PAGES, FEATS]), ALU.mult).then_inc(pages_kept, 1)
                    between(1)
                    dve.wait_ge(pages_kept, 2 * w + 2)
                    v.tensor_reduce(picked[u][:, :, :], paged[u][:, :, :, :].rearrange("p s g f -> p s f g"), X, ALU.add).then_inc(picks_ready, 1)
                    between(2)
                    dve.wait_ge(picks_ready, w + 1)
                    typed_norm = m.typed_norm[:, bass.ds(n, 1), :, :].rearrange("p a s r -> p r (a s)")
                    v.tensor_tensor(typed[u][:, :, :, :], picked[u][:, :, :].rearrange("p s f -> p f s").unsqueeze(1).broadcast_to([128, RELATIONS, FEATS, SLOTS]),
                                    typed_norm.unsqueeze(2).broadcast_to([128, RELATIONS, FEATS, SLOTS]), ALU.mult).then_inc(typed_ready, 1)
                    between(3)
                    dve.wait_ge(typed_ready, w + 1)
                    at_least(dve, rows_turned, w - PAIR + 1)
                    v.tensor_reduce(rows[u][:, :], typed[u][:, :, :, :].rearrange("p r f s -> p (r f) s"), X, ALU.add).then_inc(rows_ready, 1)

                def lap(q):
                    for i in range(MATRIX_TURNS):
                        table = TABLE_AFTER.index(i) if i in TABLE_AFTER else -1

                        def between(stage):
                            if stage == 0 and table >= 0:
                                weigh_got(q, table)
                            if stage == 1:
                                if table >= 0:
                                    sum_got(q, table)
                                make_hot(q, i + PAIR, VEC_LINES[0:1])
                            if stage == 2:
                                make_hot(q, i + PAIR, VEC_LINES[1:2])
                            if stage == 3:
                                make_hot(q, i + PAIR, VEC_LINES[2:])

                        if is_one(counted(q, i)[0]):
                            from_products(q, i, between)
                        elif table >= 0:
                            weigh_got(q, table)
                            sum_got(q, table)
                for i in range(PAIR):
                    make_hot(0, i, VEC_LINES)
                laps(dve, lap)


def finish_layer(nc, d, m, sem, k, out):
    ctx = ExitStack()
    with ctx:
        def sb(name, shape, dt=F32):
            return ctx.enter_context(nc.sbuf_tensor(f"{name}_{k}", shape, dt))

        agg = sb("agg", [NP, NB, FEATS])
        top, power, total, result = sb("top", [NP, NB]), sb("power", [NP, NB, FEATS]), sb("total", [NP, NB]), sb("result", [NP, NB, FEATS])
        t = Tensors()
        t.x, t.out = agg, result
        t.mean, t.root, t.square = sb("mean", [NP, NB]), sb("root", [NP, NB]), sb("square", [NP, NB, FEATS])
        aggs_in, chain_sem = sem(f"aggs_in{k}"), sem(f"finish_chain{k}")
        shifted, raised, totals_ready, logs_ready = sem(f"z_shifted{k}"), sem(f"z_raised{k}"), sem(f"z_totals{k}"), sem(f"z_logs{k}")
        spread_ready, root_ready, result_ready, stored = sem(f"z_spread{k}"), sem(f"z_root{k}"), sem(f"z_result{k}"), sem(f"z_stored{k}")
        wide = [NP, NB, FEATS]
        with nc.Block() as block:
            @block.gpsimd
            def _(pool):
                for b in range(NB):
                    pool.indirect_dma_start(agg[:, b, :], None, m.row_aggs[k], bass.IndirectOffsetOnAxis(m.node_last[:, b:b + 1], 0)).then_inc(aggs_in, 16)

            if k == 1:
                @block.scalar
                def _(act):
                    act.wait_ge(shifted, 1)
                    nc.scalar.activation(power[:, :, :], agg[:, :, :], ACT.Exp).then_inc(raised, 1)
                    act.wait_ge(totals_ready, 1)
                    nc.scalar.activation(total[:, :], total[:, :], ACT.Ln).then_inc(logs_ready, 1)
                    act.wait_ge(spread_ready, 1)
                    nc.scalar.activation(t.root[:, :], t.mean[:, :], ACT.Sqrt).then_inc(root_ready, 1)

                @block.sync
                def _(sp):
                    sp.wait_ge(result_ready, 1)
                    sp.dma_start(out.rearrange("(p b) f -> p b f", b=NB), result[:, :, :]).then_inc(stored, 16)
                    sp.wait_ge(stored, 16)

            @block.vector
            def _(dve):
                chain = Chain(dve, chain_sem)
                v = nc.vector
                dve.wait_ge(aggs_in, 16 * NB)
                chain(v.tensor_tensor(agg[:, :, :], agg[:, :, :], m.node_has[:, :].unsqueeze(2).broadcast_to(wide), ALU.mult))
                chain(v.tensor_tensor(agg[:, :, :], agg[:, :, :], m.rooted[:, :, :], ALU.add))
                if k == 0:
                    chain(v.tensor_scalar(m.hidden[:, :, :], agg[:, :, :], 0.0, None, ALU.max))
                    return
                chain(v.tensor_reduce(top[:, :], agg[:, :, :], X, ALU.max))
                v.tensor_tensor(agg[:, :, :], agg[:, :, :], top[:, :].unsqueeze(2).broadcast_to(wide), ALU.subtract).then_inc(shifted, 1)
                dve.wait_ge(raised, 1)
                v.tensor_reduce(total[:, :], power[:, :, :], X, ALU.add).then_inc(totals_ready, 1)
                dve.wait_ge(logs_ready, 1)
                chain(v.tensor_tensor(agg[:, :, :], agg[:, :, :], total[:, :].unsqueeze(2).broadcast_to(wide), ALU.subtract))
                chain(v.tensor_tensor(agg[:, :, :], agg[:, :, :], m.node_x[:, :, :], ALU.add))
                norm_vector(v, dve, chain, t, spread_ready, root_ready).then_inc(result_ready, 1)


def kernel(x, src, dst, edge_attr_16, edge_type_8, L0_gnn_W_msg, L0_gnn_b_msg, L0_gnn_W_attn, L0_gnn_b_attn,
           L1_gnn_W1, L1_gnn_root1, L1_gnn_b1, L1_gnn_W2, L1_gnn_root2, L1_gnn_b2):
    import numpy as np
    import concourse.bacc as bacc
    from concourse.bass_utils import run_bass_kernel_spmd as run

    efeat = np.zeros((EDGES + SLOTS, FEATS), np.float32)
    efeat[0:EDGES] = edge_attr_16
    ids = np.zeros((EDGES + SLOTS, 2), np.int32)
    ids[0:EDGES, 0] = src
    ids[0:EDGES, 1] = edge_type_8
    arrays = {
        "x": x, "dst": dst, "efeat": efeat, "ids": ids,
        "w_msg": L0_gnn_W_msg, "b_msg": L0_gnn_b_msg, "w_attn": L0_gnn_W_attn, "b_attn": L0_gnn_b_attn,
        "w1": L1_gnn_W1, "root1": L1_gnn_root1, "b1": L1_gnn_b1, "w2": L1_gnn_W2, "root2": L1_gnn_root2, "b2": L1_gnn_b2,
    }
    arrays = {f"in_{name}": np.ascontiguousarray(a) for name, a in arrays.items()}
    nc = bacc.Bacc("TRN2", target_bir_lowering=False, num_devices=1)
    given = {name[3:]: nc.dram_tensor(name, a.shape, mybir.dt.from_np(a.dtype), kind="ExternalInput").ap() for name, a in arrays.items()}
    d = Tensors()
    d.x, d.dst, d.efeat, d.ids = given["x"], given["dst"], given["efeat"], given["ids"]
    d.w_msg, d.b_msg, d.w_attn, d.b_attn = given["w_msg"], given["b_msg"], given["w_attn"], given["b_attn"]
    d.layers = [(given["w1"], given["root1"], given["b1"]), (given["w2"], given["root2"], given["b2"])]
    out = nc.dram_tensor("out", (NODES, FEATS), F32, kind="ExternalOutput").ap()
    build(nc, d, out)
    return run(nc, [arrays], core_ids=[0]).results[0]["out"]
```
